# Optimizing a Trainium2 kernel written in Bass

```python
import numpy as np
import jax
import jax.numpy as jnp

def _softmax(x, axis=-1):
    return jax.nn.softmax(x, axis=axis)

def _gelu(x):
    return jax.nn.gelu(x, approximate=True)

def _silu(x):
    return jax.nn.silu(x)

def _sigmoid(x):
    return jax.nn.sigmoid(x)

def _layernorm(x, axis=-1, eps=1e-05):
    m = jnp.mean(x, axis=axis, keepdims=True)
    v = jnp.var(x, axis=axis, keepdims=True)
    return (x - m) / jnp.sqrt(v + eps)

def _scatter_add(tgt, idx, src, axis=0):
    return tgt.at[idx].add(src)

def _segment_sum(src, seg, n):
    return jax.ops.segment_sum(src, seg, n)
kernel_name = 'mk_seq_preln_d1_jaxref_r8_d3fe8d'

def setup_inputs(seed: int=0):
    np.random.seed(seed)
    _w = jnp.asarray

    def _L0_attn_setup():
        import jax, jax.numpy as jnp
        import numpy as np
        H = 8
        LN_EPS = 1e-05
        key = jax.random.key(seed)
        ks = jax.random.split(key, 4)
        B, S, D = (4, 256, 128)
        x = jax.random.normal(ks[0], (B, S, D), dtype=jnp.float32)
        sc = 1.0 / np.sqrt(D)
        Wq = jax.random.normal(ks[1], (D, D), dtype=jnp.float32) * sc
        Wk = jax.random.normal(ks[2], (D, D), dtype=jnp.float32) * sc
        Wv = jax.random.normal(ks[3], (D, D * H), dtype=jnp.float32) * sc
        return {'x': x, 'Wq': Wq, 'bq': jnp.zeros((D,), jnp.float32), 'Wk': Wk, 'bk': jnp.zeros((D,), jnp.float32), 'Wv': Wv, 'bv': jnp.zeros((D * H,), jnp.float32), 'gamma': jnp.ones((D,), jnp.float32), 'beta': jnp.zeros((D,), jnp.float32)}
    _L0_attn_in = _L0_attn_setup()

    def _L0_ffn_setup():
        import jax, jax.numpy as jnp
        import numpy as np
        NUM_EXPERTS = 8
        TOP_K = 2
        D_MODEL = 128
        D_HID = 512
        BATCH, SEQ = (2, 256)
        key = jax.random.key(seed)
        ks = jax.random.split(key, 5)
        s = 0.02
        return {'x': jax.random.normal(ks[0], (BATCH, SEQ, D_MODEL), dtype=jnp.float32), 'Wg': jax.random.normal(ks[1], (D_MODEL, NUM_EXPERTS), dtype=jnp.float32) * s, 'bg': jnp.zeros((NUM_EXPERTS,), dtype=jnp.float32), 'W0': jax.random.normal(ks[2], (NUM_EXPERTS, D_MODEL, D_HID), dtype=jnp.float32) * s, 'b0': jnp.zeros((NUM_EXPERTS, D_HID), dtype=jnp.float32), 'W1': jax.random.normal(ks[3], (NUM_EXPERTS, D_MODEL, D_HID), dtype=jnp.float32) * s, 'b1': jnp.zeros((NUM_EXPERTS, D_HID), dtype=jnp.float32), 'W2': jax.random.normal(ks[4], (NUM_EXPERTS, D_HID, D_MODEL), dtype=jnp.float32) * s, 'b2': jnp.zeros((NUM_EXPERTS, D_MODEL), dtype=jnp.float32)}
    _L0_ffn_in = _L0_ffn_setup()
    _d = {'L0_attn_x': _L0_attn_in['x'], 'L0_attn_Wq': _L0_attn_in['Wq'], 'L0_attn_bq': _L0_attn_in['bq'], 'L0_attn_Wk': _L0_attn_in['Wk'], 'L0_attn_bk': _L0_attn_in['bk'], 'L0_attn_Wv': _L0_attn_in['Wv'], 'L0_attn_bv': _L0_attn_in['bv'], 'L0_attn_gamma': _L0_attn_in['gamma'], 'L0_attn_beta': _L0_attn_in['beta'], 'L0_ffn_Wg': _L0_ffn_in['Wg'], 'L0_ffn_bg': _L0_ffn_in['bg'], 'L0_ffn_W0': _L0_ffn_in['W0'], 'L0_ffn_b0': _L0_ffn_in['b0'], 'L0_ffn_W1': _L0_ffn_in['W1'], 'L0_ffn_b1': _L0_ffn_in['b1'], 'L0_ffn_W2': _L0_ffn_in['W2'], 'L0_ffn_b2': _L0_ffn_in['b2']}
    _x0 = _d['L0_attn_x']
    _d['L0_attn_x'] = jax.random.normal(jax.random.fold_in(jax.random.key(seed), 1), (2, 2048, 128), dtype=_x0.dtype)
    del _x0
    return _d

def reference(L0_attn_x, L0_attn_Wq, L0_attn_bq, L0_attn_Wk, L0_attn_bk, L0_attn_Wv, L0_attn_bv, L0_attn_gamma, L0_attn_beta, L0_ffn_Wg, L0_ffn_bg, L0_ffn_W0, L0_ffn_b0, L0_ffn_W1, L0_ffn_b1, L0_ffn_W2, L0_ffn_b2):

    def _L0_attn_ref(x, Wq, bq, Wk, bk, Wv, bv, gamma, beta):
        import jax, jax.numpy as jnp
        import numpy as np
        H = 8
        LN_EPS = 1e-05
        B, S, D = x.shape
        dk = D // H
        mu = jnp.mean(x, axis=-1, keepdims=True)
        var = jnp.mean(jnp.square(x - mu), axis=-1, keepdims=True)
        xn = (x - mu) * jax.lax.rsqrt(var + LN_EPS) * gamma + beta
        q = (xn @ Wq + bq).reshape(B, S, H, dk).transpose(0, 2, 1, 3)
        k = (xn @ Wk + bk).reshape(B, S, H, dk).transpose(0, 2, 1, 3)
        v = (xn @ Wv + bv).reshape(B, S, H, D).transpose(0, 2, 1, 3)
        scores = jnp.einsum('bhsd,bhtd->bhst', q, k) / jnp.sqrt(jnp.asarray(dk, x.dtype))
        p = jax.nn.softmax(scores, axis=-1)
        att = jnp.einsum('bhst,bhtd->bhsd', p, v)
        out = att.reshape(S, B, D, H).sum(axis=-1).reshape(B, S, D)
        return out

    def _L0_ffn_ref(x, Wg, bg, W0, b0, W1, b1, W2, b2):
        import jax, jax.numpy as jnp
        import numpy as np
        NUM_EXPERTS = 8
        TOP_K = 2
        D_MODEL = 128
        D_HID = 512
        BATCH, SEQ = (2, 256)
        n, s, d = x.shape
        gate_logits = x @ Wg + bg
        top_vals, top_idx = jax.lax.top_k(gate_logits, TOP_K)
        w = jax.nn.softmax(top_vals, axis=-1)
        combine = jnp.sum(jax.nn.one_hot(top_idx, NUM_EXPERTS, dtype=x.dtype) * w[..., None], axis=-2)
        xf = x.reshape(n * s, d)
        h = jnp.einsum('td,edh->eth', xf, W0) + b0[:, None, :]
        g = jax.nn.silu(jnp.einsum('td,edh->eth', xf, W1) + b1[:, None, :])
        y = jnp.einsum('eth,ehd->etd', h * g, W2) + b2[:, None, :]
        out = jnp.einsum('te,etd->td', combine.reshape(n * s, NUM_EXPERTS), y)
        return out.reshape(n, s, d)
    x = L0_attn_x
    x = x + _L0_attn_ref(_layernorm(x, axis=-1), L0_attn_Wq, L0_attn_bq, L0_attn_Wk, L0_attn_bk, L0_attn_Wv, L0_attn_bv, L0_attn_gamma, L0_attn_beta)
    x = x + _L0_ffn_ref(_layernorm(x, axis=-1), L0_ffn_Wg, L0_ffn_bg, L0_ffn_W0, L0_ffn_b0, L0_ffn_W1, L0_ffn_b1, L0_ffn_W2, L0_ffn_b2)
    return x

_drawn_inputs = setup_inputs


def setup_inputs(seed=0):
    import zlib

    import numpy as np

    out = dict(_drawn_inputs(seed))
    spreads = {'L0_attn_bq': (0.0, 0.1),
     'L0_attn_bk': (0.0, 2.0),
     'L0_attn_bv': (0.0, 0.1),
     'L0_attn_gamma': (1.0, 0.2),
     'L0_attn_beta': (0.0, 0.1),
     'L0_ffn_bg': (0.0, 0.1),
     'L0_ffn_b0': (0.0, 0.8),
     'L0_ffn_b1': (0.0, 0.8),
     'L0_ffn_b2': (0.0, 0.493)}
    factors = {'L0_ffn_W0': 6.904, 'L0_ffn_W1': 6.964, 'L0_ffn_W2': 6.312}
    for name, (base, spread) in spreads.items():
        noise = np.random.default_rng([zlib.crc32(name.encode()), seed]).standard_normal(out[name].shape)
        drawn = base * np.exp(spread * noise) if base else spread * noise
        out[name] = jnp.asarray(drawn.astype(out[name].dtype))
    for name, factor in factors.items():
        out[name] = (out[name] * factor).astype(out[name].dtype)
    return out
```

```python
from contextlib import ExitStack

import concourse.bass as bass
from concourse import mybir

ALU = mybir.AluOpType
ACT = mybir.ActivationFunctionType
AX = mybir.AxisListType
F32 = mybir.dt.float32
F32R = mybir.dt.float32r
BF16 = mybir.dt.bfloat16

P = 128
BATCH, SEQ, D = 2, 2048, 128
HEADS, DK = 8, 16
EXPERTS, HID = 8, 512
EPS = 1e-5
TOKENS = BATCH * SEQ
TILES = TOKENS // P
GROUPS = TILES // 4
NHEADS = BATCH * HEADS
PAIRS = NHEADS // 2
KEYB = SEQ // P
QC = SEQ // 512
STEPS = 2 * KEYB * QC
HSTEPS = STEPS // 2
VW = 32
PRODUCTS = ((0, 0), (0, 1), (0, 2), (1, 0), (1, 1), (2, 0))
ROWS = DK * len(PRODUCTS)
LEAD = 3
AHEAD = (KEYB + LEAD) * QC
HC = HID // P
FT = EXPERTS * HC
FIRST = 32
HI_LAG = 5
STACK_SEM = 16 * 2 * len(PRODUCTS)
MROW_SEM = 16 * 3 * 4


def wait(eng, sem, n):
    if isinstance(n, tuple):
        base, more, level = n
        if more:
            eng.reg_add(level, base, more)
        eng.wait_ge(sem, level if more else base)
    elif n > 0:
        eng.wait_ge(sem, n)


class Pair:

    def __init__(self, eng, p, bases=None):
        self.eng, self.p, self.bases = eng, p, bases

    def __call__(self, each, more):
        if isinstance(self.p, int):
            return self.p * each + more
        return self.bases[each], more, self.bases["level"]

    def number(self, each, more):
        return self.p * each + more


RATES = sorted({1, 2, 3, 4, 8, 16, 32, STEPS, STACK_SEM, MROW_SEM})


def over_pairs(eng, body):
    body(Pair(eng, 0), True, False, False)
    body(Pair(eng, 1), True, True, False)
    bases = {each: eng.alloc_register(f"pairs_times_{each}") for each in RATES}
    bases["level"] = eng.alloc_register("level")
    with eng.Fori(2, PAIRS - 1) as p:
        for each in RATES:
            eng.reg_mov(bases[each], p * each)
        body(Pair(eng, p, bases), True, True, True)
    body(Pair(eng, PAIRS - 1), True, True, True)
    body(Pair(eng, PAIRS), False, True, True)
    body(Pair(eng, PAIRS + 1), False, False, True)


def has_max(pair, s):
    return not isinstance(pair.p, int) or 2 * pair.p + (s + AHEAD) // HSTEPS < NHEADS


def setup_stage(nc, io, scratch, keep):
    (x, Wq, bq, Wk, bk, Wv, bv, gamma, beta, Wg, bg, b0, b1, b2) = io
    parts_d, values_d = scratch
    (ident, rank, bg_b, wg_h, wg_l, b0_c, b1_c, b1h_c, b2_sb, sel, comb3, exponent) = keep
    with ExitStack() as ctx:
        def sb(name, shape, dt=F32):
            return ctx.enter_context(nc.sbuf_tensor(name, shape, dt))

        def sem(name):
            return ctx.enter_context(nc.semaphore(name))

        xs = sb("xs", [P, TILES, D])
        xt = sb("xt", [P, TOKENS])
        wq, wk = sb("wq", [P, D]), sb("wk", [P, D])
        wv = sb("wv", [P, HEADS * D])
        wv_sum = sb("wv_sum", [P, D])
        bv_b = sb("bv_b", [P, HEADS * D])
        bv_sum = sb("bv_sum", [P, D])
        gamma_c, beta_c = sb("gamma_c", [P, 1]), sb("beta_c", [P, 1])
        bq_c, bk_c = sb("bq_c", [P, 1]), sb("bk_c", [P, 1])
        wg = sb("wg", [P, EXPERTS])
        b_rows = sb("b_rows", [FT, 2, P])
        stats = sb("stats", [P, TILES, 6])
        mv = sb("mv", [P, TILES, 2])
        ve = sb("ve", [P, TILES])
        rstd = sb("rstd", [P, TILES])
        part = [[sb(f"part{w}{i}", [P, BATCH, SEQ], BF16) for i in range(3)] for w in "qk"]
        qf, kf = sb("qf", [P, 2, 512]), sb("kf", [P, 2, 512])
        qr, kr = sb("qr", [P, 2, 512]), sb("kr", [P, 2, 512])
        vh = sb("vh", [P, BATCH, HEADS, KEYB, VW])
        ps_t, ps_q, ps_k, ps_v = [
            [ctx.enter_context(nc.psum_tensor(f"ps_{n}{i}", [P, 512], F32)) for i in range(2)]
            for n in "tqkv"]

        x_landed = [sem(f"x_landed{g}") for g in range(GROUPS)]
        qkw_landed, wv_landed, cols_landed = sem("qkw_landed"), sem("wv_landed"), sem("cols_landed")
        keep_landed = sem("keep_landed")
        sums_done, stats_done, mv_done, ve_done = sem("sums_done"), sem("stats_done"), sem("mv_done"), sem("ve_done")
        rstd_done, xhat_done, tr_done, xt_done = sem("rstd_done"), sem("xhat_done"), sem("tr_done"), sem("xt_done")
        q_ps, k_ps, v_ps = sem("q_ps"), sem("k_ps"), sem("v_ps")
        qf_done, q1_done, qr_done, q2_done, q3_done = [sem(f"{n}_done") for n in ("qf", "q1", "qr", "q2", "q3")]
        kf_done, k1_done, kr_done, k2_done, k3_done = [sem(f"{n}_done") for n in ("kf", "k1", "kr", "k2", "k3")]
        v_done, vh_zero, vh_one, ident_zero, ident_done, const_zero, const_done = [
            sem(n) for n in ("v_done", "vh_zero", "vh_one", "ident_zero", "ident_done", "const_zero", "const_done")]
        wgh_done, wgl_done, b_cols, b1h_done, scratch_written = [
            sem(n) for n in ("wgh_done", "wgl_done", "b_cols", "b1h_done", "scratch_written")]

        x_t = x.rearrange("b (n p) d -> p (b n) d", p=P)

        def col(v):
            return v.rearrange("(p a) -> p a", a=1)

        with nc.Block() as block:
            @block.sync
            def _(sp):
                for g in range(GROUPS):
                    sp.dma_start(xs[:, 4 * g:4 * g + 4, :], x_t[:, 4 * g:4 * g + 4, :]).then_inc(x_landed[g], 16)
                for b in range(BATCH):
                    done = GROUPS // BATCH * (b + 1)
                    for i, (sq, sk) in enumerate(((q1_done, k1_done), (q2_done, k2_done), (q3_done, k3_done))):
                        sp.wait_ge(sq, done)
                        sp.dma_start(parts_d[0, i, b], part[0][i][:, b, :]).then_inc(scratch_written, 16)
                        sp.wait_ge(sk, done)
                        sp.dma_start(parts_d[1, i, b], part[1][i][:, b, :]).then_inc(scratch_written, 16)
                    sp.wait_ge(v_done, done)
                    sp.dma_start(values_d[b].rearrange("h p v -> p h v"),
                                 vh[:, b].rearrange("p h k v -> p h (k v)")).then_inc(scratch_written, 16)
                sp.wait_ge(scratch_written, 16 * 7 * BATCH)
                sp.wait_ge(keep_landed, 16 * 4)

            @block.gpsimd
            def _(pool):
                nc.gpsimd.memset(ident[:], 0.0).then_inc(ident_zero, 1)
                pool.wait_ge(ident_zero, 1)
                nc.gpsimd.affine_select(out=ident[:], in_=ident[:], compare_op=ALU.not_equal, fill=1.0, base=0,
                                        pattern=[[-1, P]], channel_multiplier=1).then_inc(ident_done, 1)
                nc.gpsimd.memset(exponent[:], -0.5).then_inc(const_done, 1)
                nc.gpsimd.memset(vh[:, :, :, :, DK + 1:VW], 0.0).then_inc(vh_one, 1)
                nc.gpsimd.memset(vh[:, :, :, :, DK:DK + 1], 1.0).then_inc(vh_one, 1)
                pool.wait_ge(const_done, 1)

                def rsqrt(g):
                    pool.wait_ge(ve_done, g + 1)
                    nc.gpsimd.tensor_tensor(rstd[:, 4 * g:4 * g + 4], ve[:, 4 * g:4 * g + 4],
                                            exponent[:, 0:4], ALU.pow).then_inc(rstd_done, 1)

                rsqrt(0)
                for g in range(GROUPS):
                    if g + 1 < GROUPS:
                        rsqrt(g + 1)
                    b, c = g // 4, 512 * (g % 4)
                    pool.wait_ge(k1_done, g + 1)
                    nc.gpsimd.tensor_tensor(kr[:, g % 2, :], kf[:, g % 2, :], part[1][0][:, b, c:c + 512],
                                            ALU.subtract).then_inc(kr_done, 1)
                    pool.wait_ge(k2_done, g + 1)
                    nc.gpsimd.tensor_tensor(part[1][2][:, b, c:c + 512], kr[:, g % 2, :],
                                            part[1][1][:, b, c:c + 512], ALU.subtract).then_inc(k3_done, 1)
                nc.gpsimd.memset(sel[:], 0.0).then_inc(const_zero, 1)
                nc.gpsimd.memset(comb3[:], 0.0)
                for e in range(EXPERTS):
                    nc.gpsimd.memset(rank[:, :, e:e + 1], float(EXPERTS - e))
                for part_no in range(3):
                    pool.wait_ge(const_zero, part_no + 1)
                    nc.gpsimd.affine_select(out=sel[:], in_=sel[:], compare_op=ALU.not_equal, fill=1.0,
                                            base=-32 * part_no, pattern=[[-1, EXPERTS], [0, P]],
                                            channel_multiplier=1).then_inc(const_zero, 1)
                pool.wait_ge(const_zero, 4)

            @block.scalar
            def _(act):
                act.dma_start(wq[:], Wq).then_inc(qkw_landed, 16)
                act.dma_start(wk[:], Wk).then_inc(qkw_landed, 16)
                for dst, src in ((gamma_c, gamma), (beta_c, beta), (bq_c, bq), (bk_c, bk)):
                    act.dma_start(dst[:], col(src)).then_inc(cols_landed, 16)
                act.dma_start(wg[:], Wg).then_inc(cols_landed, 16)
                act.dma_start(wv[:], Wv).then_inc(wv_landed, 16)
                act.dma_start(bv_b[:], bv.partition_broadcast(P)).then_inc(wv_landed, 16)
                act.dma_start(bg_b[:], bg.partition_broadcast(P)).then_inc(keep_landed, 16)
                act.dma_start(b_rows[:, 0, :], b0.rearrange("e (c p) -> (e c) p", p=P)).then_inc(keep_landed, 16)
                act.dma_start(b_rows[:, 1, :], b1.rearrange("e (c p) -> (e c) p", p=P)).then_inc(keep_landed, 16)
                act.dma_start(b2_sb[:], b2).then_inc(keep_landed, 16)
                act.wait_ge(cols_landed, 16 * 5)

                def norm_out(g):
                    act.wait_ge(tr_done, g + 1)
                    nc.scalar.activation(xt[:, 512 * g:512 * g + 512], ps_t[g % 2][:], ACT.Identity,
                                         bias=beta_c[:], scale=gamma_c[:]).then_inc(xt_done, 1)

                norm_out(0)
                for g in range(GROUPS):
                    if g + 1 < GROUPS:
                        norm_out(g + 1)
                    b, c = g // 4, 512 * (g % 4)
                    act.wait_ge(k_ps, g + 1)
                    if g >= 2:
                        act.wait_ge(kr_done, g - 1)
                    nc.scalar.activation(kf[:, g % 2, :], ps_k[g % 2][:], ACT.Identity,
                                         bias=bk_c[:]).then_inc(kf_done, 1)
                    act.wait_ge(qf_done, g + 1)
                    nc.scalar.activation(part[0][0][:, b, c:c + 512], qf[:, g % 2, :], ACT.Copy).then_inc(q1_done, 1)
                    act.wait_ge(kf_done, g + 1)
                    nc.scalar.activation(part[1][0][:, b, c:c + 512], kf[:, g % 2, :], ACT.Copy).then_inc(k1_done, 1)
                    act.wait_ge(qr_done, g + 1)
                    nc.scalar.activation(part[0][1][:, b, c:c + 512], qr[:, g % 2, :], ACT.Copy).then_inc(q2_done, 1)
                    act.wait_ge(kr_done, g + 1)
                    nc.scalar.activation(part[1][1][:, b, c:c + 512], kr[:, g % 2, :], ACT.Copy).then_inc(k2_done, 1)
                act.wait_ge(b_cols, 1)
                nc.scalar.activation(b0_c[:], ps_t[0][:, 0:FT], ACT.Copy)
                nc.scalar.activation(b1_c[:], ps_t[0][:, FT:2 * FT], ACT.Copy)
                nc.scalar.mul(b1h_c[:], ps_t[0][:, FT:2 * FT], 0.5).then_inc(b1h_done, 1)

            @block.vector
            def _(dve):
                def moments(g):
                    dve.wait_ge(x_landed[g], 16)
                    for j in range(4 * g, 4 * g + 4):
                        last = nc.vector.bn_stats(stats[:, j, :], xs[:, j, :])
                    last.then_inc(stats_done, 1)
                    dve.wait_ge(stats_done, g + 1)
                    for j in range(4 * g, 4 * g + 4):
                        last = nc.vector.bn_aggr(mv[:, j, :], stats[:, j, :])
                    last.then_inc(mv_done, 1)
                    dve.wait_ge(mv_done, g + 1)
                    nc.vector.tensor_scalar(ve[:, 4 * g:4 * g + 4], mv[:, 4 * g:4 * g + 4, 1], 1.0 + EPS, EPS * EPS,
                                            ALU.mult, ALU.add).then_inc(ve_done, 1)

                def normalise(g):
                    dve.wait_ge(rstd_done, g + 1)
                    for j in range(4 * g, 4 * g + 4):
                        last = nc.vector.tensor_scalar(xs[:, j, :], xs[:, j, :], mv[:, j, 0:1], rstd[:, j:j + 1],
                                                       ALU.subtract, ALU.mult)
                    last.then_inc(xhat_done, 1)

                def queries_and_values(g):
                    b, c = g // 4, 512 * (g % 4)
                    dve.wait_ge(q_ps, g + 1)
                    if g >= 2:
                        dve.wait_ge(q1_done, g - 1)
                        dve.wait_ge(qr_done, g - 1)
                    nc.vector.tensor_scalar(qf[:, g % 2, :], ps_q[g % 2][:], bq_c[:], float(DK) ** -0.5,
                                            ALU.add, ALU.mult).then_inc(qf_done, 1)
                    dve.wait_ge(v_ps, g + 1)
                    for j in range(4):
                        last = nc.vector.tensor_tensor(
                            vh[:, b, :, 4 * (g % 4) + j, 0:DK],
                            ps_v[g % 2][:, D * j:D * j + D].rearrange("p (h v) -> p h v", v=DK),
                            bv_sum[:].rearrange("p (h v) -> p h v", v=DK), ALU.add)
                    last.then_inc(v_done, 1)
                    dve.wait_ge(q1_done, g + 1)
                    if g >= 2:
                        dve.wait_ge(q2_done, g - 1)
                        dve.wait_ge(q3_done, g - 1)
                    nc.vector.tensor_tensor(qr[:, g % 2, :], qf[:, g % 2, :], part[0][0][:, b, c:c + 512],
                                            ALU.subtract).then_inc(qr_done, 1)
                    dve.wait_ge(q2_done, g + 1)
                    dve.wait_ge(qr_done, g + 1)
                    nc.vector.tensor_tensor(part[0][2][:, b, c:c + 512], qr[:, g % 2, :],
                                            part[0][1][:, b, c:c + 512], ALU.subtract).then_inc(q3_done, 1)

                moments(0)
                dve.wait_ge(wv_landed, 32)
                nc.vector.tensor_reduce(wv_sum[:], wv[:].rearrange("p (j n) -> p j n", n=HEADS), AX.X,
                                        ALU.add).then_inc(sums_done, 1)
                nc.vector.tensor_reduce(bv_sum[:], bv_b[:].rearrange("p (j n) -> p j n", n=HEADS), AX.X,
                                        ALU.add).then_inc(sums_done, 1)
                dve.wait_ge(cols_landed, 16 * 5)
                nc.vector.tensor_copy(wg_h[:], wg[:]).then_inc(wgh_done, 1)
                moments(1)
                normalise(0)
                dve.wait_ge(sums_done, 2)
                dve.wait_ge(vh_one, 2)
                for g in range(GROUPS):
                    if g + 2 < GROUPS:
                        moments(g + 2)
                    if g + 1 < GROUPS:
                        normalise(g + 1)
                    queries_and_values(g)
                dve.wait_ge(wgh_done, 1)
                nc.vector.tensor_tensor(wg_l[:], wg[:], wg_h[:].bitcast(F32), ALU.subtract).then_inc(wgl_done, 1)
                dve.wait_ge(wgl_done, 1)

            @block.tensor
            def _(pe):
                def transposes(g):
                    pe.wait_ge(xhat_done, g + 1)
                    if g >= 2:
                        pe.wait_ge(xt_done, g - 1)
                    for j in range(4):
                        last = nc.tensor.transpose(ps_t[g % 2][:, P * j:P * j + P], xs[:, 4 * g + j, :], ident[:])
                    last.then_inc(tr_done, 1)

                pe.wait_ge(ident_done, 1)
                transposes(0)
                pe.wait_ge(qkw_landed, 32)
                pe.wait_ge(sums_done, 1)
                for g in range(GROUPS):
                    if g + 1 < GROUPS:
                        transposes(g + 1)
                    pe.wait_ge(xt_done, g + 1)
                    if g >= 2:
                        pe.wait_ge(kf_done, g - 1)
                    nc.tensor.matmul(ps_k[g % 2][:], wk[:], xt[:, 512 * g:512 * g + 512], start=True,
                                     stop=True).then_inc(k_ps, 1)
                    if g >= 2:
                        pe.wait_ge(qf_done, g - 1)
                    nc.tensor.matmul(ps_q[g % 2][:], wq[:], xt[:, 512 * g:512 * g + 512], start=True,
                                     stop=True).then_inc(q_ps, 1)
                    if g >= 2:
                        pe.wait_ge(v_done, g - 1)
                    for j in range(4):
                        last = nc.tensor.matmul(ps_v[g % 2][:, P * j:P * j + P],
                                                xt[:, 512 * g + P * j:512 * g + P * j + P], wv_sum[:],
                                                start=True, stop=True)
                    last.then_inc(v_ps, 1)
                pe.wait_ge(keep_landed, 16 * 4)
                for i in range(2):
                    last = nc.tensor.transpose(ps_t[0][:, FT * i:FT * i + FT], b_rows[:, i, :], ident[0:FT, 0:FT])
                last.then_inc(b_cols, 1)


def main_stage(nc, x, weights, out, scratch, keep):
    parts_d, values_d = scratch
    (ident, rank, bg_b, wg_h, wg_l, b0_c, b1_c, b1h_c, b2_sb, sel, comb3, exponent) = keep
    W0, W1, W2 = weights
    with ExitStack() as ctx:
        def sb(name, shape, dt=F32):
            return ctx.enter_context(nc.sbuf_tensor(name, shape, dt))

        def sem(name):
            return ctx.enter_context(nc.semaphore(name))

        w_h = [sb(f"w{i}_h", [P, EXPERTS, 512], F32R) for i in range(3)]
        w_l = [sb(f"w{i}_l", [P, EXPERTS, 512], F32R) for i in range(3)]
        w_raw = sb("w_raw", [P, 2, 512])
        q_max, k_max = sb("q_max", [P, 2, SEQ], BF16), sb("k_max", [P, 2, SEQ], BF16)
        q_exp, k_exp = sb("q_exp", [P, 2, SEQ], BF16), sb("k_exp", [P, 2, SEQ], BF16)
        values = sb("values", [P, 2, KEYB, VW])
        blockmax = sb("blockmax", [P, 2, KEYB, QC])
        rowmax = sb("rowmax", [P, 32])
        rowmax_t = sb("rowmax_t", [P, 32])
        negmax = sb("negmax", [P, 32])
        negmax_r = sb("negmax_r", [P, 32])
        m_parts = sb("m_parts", [P, 2, 3, 32], BF16)
        probs = sb("probs", [P, 2, QC, 512])
        o_sb = sb("o_sb", [P, 2, 512])
        x_in = sb("x_in", [P, 4, D])
        x_res = sb("x_res", [P, 4, D])
        x_hat = sb("x_hat", [P, 4, D])
        inv_den = sb("inv_den", [P, 8, 4])
        stats = sb("stats2", [P, 4, 6])
        mv = sb("mv2", [P, 4, 2])
        ve = sb("ve2", [P, 4])
        rstd = sb("rstd2", [P, 4])
        xt_h, xt_l = sb("xt_h", [P, 512], F32R), sb("xt_l", [P, 512], F32R)
        logits = sb("logits", [P, 4, EXPERTS])
        top1, top2, rank1, rank2 = [sb(n, [P, 4]) for n in ("top1", "top2", "rank1", "rank2")]
        hit1, hit2, sel1, sel2, rest = [sb(n, [P, 4, EXPERTS]) for n in ("hit1", "hit2", "sel1", "sel2", "rest")]
        gap, gap_exp, gate_sum, gate1, gate2 = [sb(n, [P, 4]) for n in ("gap", "gap_exp", "gate_sum", "gate1", "gate2")]
        comb = sb("comb", [P, 4, EXPERTS])
        comb_t = x_in[0:EXPERTS].rearrange("p c d -> p (c d)")
        comb_b = sb("comb_b", [P, EXPERTS, 512])
        hid, gate = sb("hid", [P, 2, 512]), sb("gate", [P, 2, 512])
        comb_m = gate[0:EXPERTS, 0, 0:256].bitcast(BF16)
        hid_h, hid_l = sb("hid_h", [P, 2, 512], F32R), sb("hid_l", [P, 2, 512], F32R)
        y_sum, y_scaled = w_raw[:, 0, :], w_raw[:, 1, :]
        comb_r = y_scaled[0:EXPERTS, :]
        out_sb = sb("out_sb", [P, 4, D])

        ps_s = [ctx.enter_context(nc.psum_tensor(f"ps_s{i}", [P, 512], F32)) for i in range(2)]
        ps_m = [ctx.enter_context(nc.psum_tensor(f"ps_m{i}", [P, 512], F32)) for i in range(2)]
        ps_o, ps_g, ps_u, ps_y = [ctx.enter_context(nc.psum_tensor(n, [P, 512], F32))
                                  for n in ("ps_o", "ps_g", "ps_u", "ps_y")]
        bcast_banks = (ps_g, ps_u, ps_y)

        max_landed = [sem(f"max_landed{i}") for i in range(2)]
        exp_landed = [sem(f"exp_landed{i}") for i in range(2)]
        values_landed = [sem(f"values_landed{i}") for i in range(2)]
        mrow_landed = [sem(f"mrow_landed{i}") for i in range(2)]
        ones_done, max_ps, max_done = sem("ones_done"), sem("max_ps"), sem("max_done")
        fold_done, fold_t, neg_done, m1_done, negr_done, m2_done, m_ready = [
            sem(n) for n in ("fold_done", "fold_t", "neg_done", "m1_done", "negr_done", "m2_done", "m_ready")]
        score_ps, probs_done, pv_done, o_done = sem("score_ps"), sem("probs_done"), sem("pv_done"), sem("o_done")
        w_landed = [sem(f"w_landed{i}") for i in range(2)]
        wh_done, w_done = sem("wh_done"), sem("w_done")
        names = ("xin_landed o_turned den_done att_done xres_done st_done mv_done ve_done rs_done xhat_done xt_ps "
                 "xth_done xtl_done logit_ps logit_done top1_done hit1_done pick1_done rank1_done sel1_done "
                 "rest_done top2_done hit2_done pick2_done rank2_done sel2_done gap_done gexp_done gsum_done "
                 "gate1_done gate2_done mix1_done mix2_done comb_done comb_ps comb_t_done comb1_done comb_r_done "
                 "comb2_done comb3_done b2_ps y_init bcast_ps bcast_done gate_ps up_ps tanh_done gate_done "
                 "silu_done hid_done hi_done lo_done y_ps y_scaled_done y_done final_ps base_done out_done").split()
        S = {n: sem("e_" + n) for n in names}
        out_stored = sem("out_stored")

        x_pairs = x.rearrange("b s d -> (b s) d").rearrange("(f h c q) d -> f h q c d", h=2, c=4, q=64)
        out_pairs = out.rearrange("b s d -> (b s) d").rearrange("(f h c q) d -> f h q c d", h=2, c=4, q=64)
        parts_h = parts_d.rearrange("w i b (h k) s -> w i (b h) k s", k=DK)
        values_h = values_d.rearrange("b h p v -> (b h) p v")

        block = ctx.enter_context(nc.Block())

        @block.sync
        def _(sp):
            def load_stack(q, k, par, head, landed):
                for i, (a, b) in enumerate(PRODUCTS):
                    sp.dma_start(q[DK * i:DK * i + DK, par, :], parts_h[0, a, head]).then_inc(landed[par], 16)
                    sp.dma_start(k[DK * i:DK * i + DK, par, :], parts_h[1, b, head]).then_inc(landed[par], 16)

            def load_for_max(pair, h):
                wait(sp, max_ps, pair(STEPS, HSTEPS * (h - 1)))
                load_stack(q_max, k_max, h % 2, pair.number(2, h), max_landed)

            def load_for_exp(pair, h):
                wait(sp, score_ps, pair(STEPS, HSTEPS * (h - 1)))
                load_stack(q_exp, k_exp, h % 2, pair.number(2, h), exp_landed)
                wait(sp, pv_done, pair(2 * KEYB, KEYB * (h - 1)))
                sp.dma_start(values[:, h % 2].rearrange("p k v -> p (k v)"),
                             values_h[pair.number(2, h)]).then_inc(values_landed[h % 2], 16)

            def load_m_rows(pair, h):
                wait(sp, m_ready, pair(2, h + 1))
                for i in range(3):
                    row = q_exp[ROWS + i:ROWS + i + 1, h % 2, :].rearrange("a (c q s) -> a q c s", q=4, s=32)
                    for q in range(4):
                        sp.dma_start(row[:, q], m_parts[32 * q:32 * q + KEYB, h % 2, i, :]
                                     ).then_inc(mrow_landed[h % 2], 16)

            def body(pair, attention, experts, tail):
                if experts:
                    wait(sp, S["comb3_done"], pair(2, -2))
                    for h in range(2):
                        sp.dma_start(x_in[64 * h:64 * h + 64], x_pairs[pair.number(1, -1), h]
                                     ).then_inc(S["xin_landed"], 16)
                last = isinstance(pair.p, int) and pair.p == PAIRS - 1
                if attention:
                    if not last:
                        load_for_max(pair, 2)
                    load_for_exp(pair, 1)
                if tail:
                    wait(sp, S["out_done"], pair(1, -1))
                    for h in range(2):
                        sp.dma_start(out_pairs[pair.number(1, -2), h], out_sb[64 * h:64 * h + 64]
                                     ).then_inc(out_stored, 16)
                if attention:
                    load_m_rows(pair, 1)
                    if not last:
                        load_for_max(pair, 3)
                        load_for_exp(pair, 2)
                        load_m_rows(pair, 2)

            start = Pair(sp, 0)
            load_for_max(start, 0)
            load_for_max(start, 1)
            load_for_exp(start, 0)
            load_m_rows(start, 0)
            over_pairs(sp, body)
            sp.wait_ge(out_stored, 32 * PAIRS)

        @block.tensor
        def _(pe):
            def max_block(pair, s):
                head, par = s // HSTEPS, s // HSTEPS % 2
                c, j = s % HSTEPS // QC, s % QC
                if s % HSTEPS == 0:
                    wait(pe, max_landed[par], pair(STACK_SEM, STACK_SEM * (head // 2 + 1)))
                wait(pe, max_done, pair(STEPS, s - 1))
                nc.tensor.matmul(ps_m[s % 2][:], q_max[0:ROWS, par, P * c:P * c + P],
                                 k_max[0:ROWS, par, 512 * j:512 * j + 512], start=True,
                                 stop=True).then_inc(max_ps, 1)

            def score_block(pair, s):
                par, t, j = s // HSTEPS, s % HSTEPS // QC, s % QC
                if s % HSTEPS == 0:
                    wait(pe, exp_landed[par], pair(STACK_SEM, STACK_SEM))
                    wait(pe, mrow_landed[par], pair(MROW_SEM, MROW_SEM))
                wait(pe, probs_done, pair(STEPS, s - 1))
                nc.tensor.matmul(ps_s[s % 2][:], k_exp[0:ROWS + 3, par, P * t:P * t + P],
                                 q_exp[0:ROWS + 3, par, 512 * j:512 * j + 512], start=True,
                                 stop=True).then_inc(score_ps, 1)

            def value_products(pair, k):
                par, t = k // KEYB % 2, k % KEYB
                if t == 0:
                    wait(pe, values_landed[par], pair(16, 16))
                    wait(pe, o_done, pair(2, k // KEYB))
                wait(pe, probs_done, pair(STEPS, QC * k + QC))
                for j in range(QC):
                    last = nc.tensor.matmul(ps_o[VW * j:VW * j + VW, :], values[:, par, t, :],
                                            probs[:, k % 2, j, :], start=(t == 0), stop=(t == KEYB - 1),
                                            tile_position=(0, VW * j))
                last.then_inc(pv_done, 1)

            def product(ps, wh, wl, ah, al, start, stop):
                nc.tensor.matmul(ps, wh, ah, start=start, stop=False)
                nc.tensor.matmul(ps, wl, ah, start=False, stop=False)
                return nc.tensor.matmul(ps, wh, al, start=False, stop=stop)

            def expert_steps(f, t, back):
                def at(each, more):
                    return f(each, more - back * each)

                if t == 4:
                    wait(pe, o_done, at(2, 2))
                    wait(pe, S["gate_done"], at(FT, 0))
                    wait(pe, S["hid_done"], at(FT, 0))
                    turned = o_sb[:].rearrange("p h (q a) -> p a h q", a=8)
                    for a in range(8):
                        last = nc.tensor.transpose((ps_g, ps_u)[a // 4][:, P * (a % 4):P * (a % 4) + P],
                                                   turned[:, a], ident[:])
                    last.then_inc(S["o_turned"], 1)
                if t == 13:
                    wait(pe, S["xhat_done"], at(1, 1))
                    wait(pe, S["out_done"], at(1, 0))
                    for c in range(4):
                        last = nc.tensor.transpose(ps_y[:, P * c:P * c + P], x_hat[:, c, :], ident[:])
                    last.then_inc(S["xt_ps"], 1)
                if t == 15:
                    wait(pe, S["xth_done"], at(1, 1))
                    wait(pe, S["xtl_done"], at(1, 1))
                    for c in range(4):
                        for i, (a, w) in enumerate(((xt_h, wg_h), (xt_h, wg_l), (xt_l, wg_h), (xt_l, wg_l))):
                            last = nc.tensor.matmul(ps_g[:, EXPERTS * c:EXPERTS * c + EXPERTS],
                                                    a[:, P * c:P * c + P], w[:], start=(i == 0), stop=(i == 3))
                    last.then_inc(S["logit_ps"], 1)
                if t == 25:
                    wait(pe, S["comb_done"], at(1, 1))
                    for c in range(4):
                        last = nc.tensor.transpose(ps_u[0:EXPERTS, P * c:P * c + P], comb[:, c, :], ident[:])
                    last.then_inc(S["comb_ps"], 1)
                if t == 27:
                    wait(pe, S["comb_t_done"], at(1, 1))
                    nc.tensor.matmul(ps_y[:], b2_sb[:], comb_t, start=True, stop=True).then_inc(S["b2_ps"], 1)
                if 29 <= t < 32:
                    for e in range(3 * (t - 29), min(3 * (t - 29) + 3, EXPERTS)):
                        if e == 0:
                            wait(pe, S["comb3_done"], at(2, 2))
                        if e == 2:
                            wait(pe, S["y_init"], at(1, 1))
                        if e >= 3:
                            wait(pe, S["bcast_done"], at(EXPERTS, e - 2))
                        nc.tensor.matmul(bcast_banks[e % 3][:], sel[:, e, :], comb3[:], start=True,
                                         stop=True).then_inc(S["bcast_ps"], 1)
                n, kind = (t - FIRST) // 3, (t - FIRST) % 3
                if 0 <= n < FT and kind == 0:
                    e, c = n // HC, P * (n % HC)
                    if n == 0:
                        wait(pe, S["bcast_done"], at(EXPERTS, 7))
                        if isinstance(f.p, int) and f.p == 1:
                            wait(pe, w_done, 3 * EXPERTS)
                    else:
                        wait(pe, S["gate_done"], at(FT, n))
                    product(ps_g[:], w_h[1][:, e, c:c + P], w_l[1][:, e, c:c + P], xt_h[:], xt_l[:],
                            True, True).then_inc(S["gate_ps"], 1)
                if 0 <= n < FT and kind == 1:
                    e, c = n // HC, P * (n % HC)
                    if n == 0:
                        wait(pe, S["bcast_done"], at(EXPERTS, 8))
                    else:
                        wait(pe, S["hid_done"], at(FT, n))
                    product(ps_u[:], w_h[0][:, e, c:c + P], w_l[0][:, e, c:c + P], xt_h[:], xt_l[:],
                            True, True).then_inc(S["up_ps"], 1)
                m = n - 2
                if 0 <= m < FT and kind == 2:
                    e, c = m // HC, m % HC
                    if c == 0:
                        if e == 0:
                            wait(pe, S["bcast_done"], at(EXPERTS, 6))
                        else:
                            wait(pe, S["y_scaled_done"], at(EXPERTS, e))
                    wait(pe, S["hi_done"], at(FT, m + 1))
                    wait(pe, S["lo_done"], at(FT, m + 1))
                    product(ps_y[:], w_h[2][:, e, P * c:P * c + P], w_l[2][:, e, P * c:P * c + P],
                            hid_h[:, m % 2, :], hid_l[:, m % 2, :], c == 0, c == HC - 1).then_inc(S["y_ps"], 1)
                if t == STEPS + 10:
                    wait(pe, S["y_done"], at(EXPERTS, EXPERTS))
                    for c in range(4):
                        last = nc.tensor.transpose(ps_y[:, P * c:P * c + P], y_sum[:, P * c:P * c + P], ident[:])
                    last.then_inc(S["final_ps"], 1)

            def body(pair, attention, experts, tail):
                for s in range(STEPS):
                    if attention:
                        score_block(pair, s)
                        if has_max(pair, s):
                            max_block(pair, s + AHEAD)
                    if s % QC == 0 and (s > 0 and attention or s == 0 and experts):
                        value_products(pair, s // QC - 1)
                    if tail:
                        expert_steps(pair, s + STEPS, 2)
                    if experts:
                        expert_steps(pair, s, 1)

            pe.wait_ge(ones_done, 2)
            for s in range(AHEAD):
                max_block(Pair(pe, 0), s)
            over_pairs(pe, body)

        @block.scalar
        def _(act):
            def exponentials(pair, s):
                k, j = s // QC, s % QC
                wait(act, score_ps, pair(STEPS, s + 1))
                if j == 0:
                    wait(act, pv_done, pair(2 * KEYB, k - 1))
                nc.scalar.activation(probs[:, k % 2, j, :], ps_s[s % 2][:], ACT.Exp).then_inc(probs_done, 1)

            def copy_sums(pair, h):
                wait(act, pv_done, pair(2 * KEYB, KEYB * (h + 1)))
                wait(act, S["o_turned"], pair(1, 0 if h == 0 else -1))
                nc.scalar.activation(o_sb[:, h % 2, :], ps_o[:], ACT.Copy).then_inc(o_done, 1)

            def expert_steps(f, t, back):
                def at(each, more):
                    return f(each, more - back * each)

                if t == 13:
                    wait(act, S["xt_ps"], at(1, 1))
                    nc.scalar.activation(xt_h[:], ps_y[:], ACT.Copy).then_inc(S["xth_done"], 1)
                if t == 21:
                    wait(act, S["gap_done"], at(1, 1))
                    nc.scalar.activation(gap_exp[:], gap[:], ACT.Exp).then_inc(S["gexp_done"], 1)
                if t == 28:
                    wait(act, S["b2_ps"], at(1, 1))
                    act.wait_ge(w_done, 3 * EXPERTS)
                    nc.scalar.activation(y_sum, ps_y[:], ACT.Copy).then_inc(S["y_init"], 1)
                if 29 <= t < 32:
                    for e in range(3 * (t - 29), min(3 * (t - 29) + 3, EXPERTS)):
                        wait(act, S["bcast_ps"], at(EXPERTS, e + 1))
                        nc.scalar.activation(comb_b[:, e, :], bcast_banks[e % 3][:], ACT.Copy,
                                             scale=0.5).then_inc(S["bcast_done"], 1)
                if t == 100:
                    wait(act, S["xres_done"], at(1, 1))
                    wait(act, out_stored, at(32, 0))
                    nc.scalar.activation(out_sb[:], x_res[:], ACT.Copy).then_inc(S["base_done"], 1)
                n = (t - FIRST - HI_LAG) // 3
                if 0 <= n < FT and (t - FIRST - HI_LAG) % 3 == 0:
                    wait(act, S["hid_done"], at(FT, n + 1))
                    wait(act, S["y_ps"], at(FT, n - 1))
                    nc.scalar.activation(hid_h[:, n % 2, :], hid[:, n % 2, :], ACT.Copy).then_inc(S["hi_done"], 1)

            def gate_steps(f, t, back):
                def at(each, more):
                    return f(each, more - back * each)

                n = (t - FIRST - 1) // 3
                if 0 <= n < FT and (t - FIRST) % 3 == 1:
                    wait(act, S["gate_ps"], at(FT, n + 1))
                    wait(act, S["lo_done"], at(FT, n - 1))
                    nc.scalar.activation(hid[:, n % 2, :], ps_g[:], ACT.Tanh, bias=b1h_c[:, n:n + 1],
                                         scale=0.5).then_inc(S["tanh_done"], 1)
                    wait(act, S["silu_done"], at(FT, n - 1))
                    nc.scalar.activation(gate[:, n % 2, :], ps_g[:], ACT.Identity, bias=b1_c[:, n:n + 1]
                                         ).then_inc(S["gate_done"], 1)

            def body(pair, attention, experts, tail):
                for s in range(STEPS):
                    if experts:
                        gate_steps(pair, s, 1)
                    if attention:
                        exponentials(pair, s)
                    if tail:
                        expert_steps(pair, s + STEPS, 2)
                    if experts:
                        expert_steps(pair, s, 1)
                    if s == 1 and experts:
                        copy_sums(pair, -1)
                    if s == HSTEPS + 1 and attention:
                        copy_sums(pair, 0)

            over_pairs(act, body)

        @block.vector
        def _(dve):
            def max_step(pair, s):
                head, c, j = s // HSTEPS, s % HSTEPS // QC, s % QC
                par = head % 2
                wait(dve, max_ps, pair(STEPS, s + 1))
                if s % HSTEPS == 0:
                    wait(dve, fold_done, pair(2, head - 1))
                nc.vector.tensor_reduce(blockmax[:, par, c, j:j + 1], ps_m[s % 2][:], AX.X,
                                        ALU.max).then_inc(max_done, 1)

            def row_maxima(pair, head, step):
                par = head % 2
                if step == 0:
                    wait(dve, max_done, pair(STEPS, HSTEPS * (head + 1)))
                    wait(dve, fold_t, pair(2, head))
                    nc.vector.tensor_reduce(rowmax[:, 0:KEYB], blockmax[:, par], AX.X, ALU.max).then_inc(fold_done, 1)
                    wait(dve, fold_done, pair(2, head + 1))
                    wait(dve, negr_done, pair(2, head))
                    nc.vector.transpose(rowmax_t[:], rowmax[:]).then_inc(fold_t, 1)
                if step == 1:
                    wait(dve, fold_t, pair(2, head + 1))
                    wait(dve, m_ready, pair(2, head))
                    nc.vector.tensor_scalar(negmax[:], rowmax_t[:], -1.0, None, ALU.mult).then_inc(neg_done, 1)
                    wait(dve, neg_done, pair(2, head + 1))
                    wait(dve, mrow_landed[par], pair(MROW_SEM, MROW_SEM * (head // 2)))
                    nc.vector.tensor_copy(m_parts[:, par, 0, :], negmax[:]).then_inc(m1_done, 1)
                if step == 2:
                    wait(dve, m1_done, pair(2, head + 1))
                    nc.vector.tensor_tensor(negmax_r[:], negmax[:], m_parts[:, par, 0, :],
                                            ALU.subtract).then_inc(negr_done, 1)
                    wait(dve, negr_done, pair(2, head + 1))
                    nc.vector.tensor_copy(m_parts[:, par, 1, :], negmax_r[:]).then_inc(m2_done, 1)
                if step == 3:
                    wait(dve, m2_done, pair(2, head + 1))
                    nc.vector.tensor_tensor(m_parts[:, par, 2, :], negmax_r[:], m_parts[:, par, 1, :],
                                            ALU.subtract).then_inc(m_ready, 1)

            def per_tile(v):
                return v[:].unsqueeze(2).to_broadcast([P, 4, EXPERTS])

            def expert_steps(f, t, back):
                def at(each, more):
                    return f(each, more - back * each)

                def after(name, each=1, more=1):
                    wait(dve, S[name], at(each, more))

                vec = nc.vector
                tt, ts = nc.vector.tensor_tensor, nc.vector.tensor_scalar
                if t == 5:
                    after("o_turned")
                    for i, ps in enumerate((ps_g, ps_u)):
                        den = ps[:].rearrange("p (a c j) -> p a c j", a=4, j=VW)[:, :, :, DK]
                        last = vec.reciprocal(inv_den[:, 4 * i:4 * i + 4, :], den)
                    last.then_inc(S["den_done"], 1)
                if t == 6:
                    after("den_done")
                    for i, ps in enumerate((ps_g, ps_u)):
                        sums = ps[:].rearrange("p (a c j) -> p a c j", a=4, j=VW)
                        dst = x_hat[:].rearrange("p c (a j) -> p a c j", j=DK)
                        for a in range(4):
                            inv = inv_den[:, 4 * i + a, :].unsqueeze(2).to_broadcast([P, 4, DK])
                            last = tt(dst[:, 4 * i + a], sums[:, a, :, 0:DK], inv, ALU.mult)
                    last.then_inc(S["att_done"], 1)
                if t == 7:
                    after("att_done")
                    after("base_done", 1, 0)
                    after("xin_landed", 32, 32)
                    tt(x_res[:], x_hat[:], x_in[:], ALU.add).then_inc(S["xres_done"], 1)
                if t == 8:
                    after("xres_done")
                    for c in range(4):
                        last = vec.bn_stats(stats[:, c, :], x_res[:, c, :])
                    last.then_inc(S["st_done"], 1)
                if t == 9:
                    for c in range(4):
                        last = vec.bn_aggr(mv[:, c, :], stats[:, c, :])
                    last.then_inc(S["mv_done"], 1)
                if t == 10:
                    after("mv_done")
                    ts(ve[:], mv[:, :, 1], EPS, None, ALU.add).then_inc(S["ve_done"], 1)
                if t == 12:
                    after("rs_done")
                    for c in range(4):
                        last = ts(x_hat[:, c, :], x_res[:, c, :], mv[:, c, 0:1], rstd[:, c:c + 1],
                                  ALU.subtract, ALU.mult)
                    last.then_inc(S["xhat_done"], 1)
                if t == 14:
                    after("xth_done")
                    tt(xt_l[:], ps_y[:], xt_h[:].bitcast(F32), ALU.subtract).then_inc(S["xtl_done"], 1)
                if t == 16:
                    after("logit_ps")
                    tt(logits[:], ps_g[:, 0:4 * EXPERTS].rearrange("p (c e) -> p c e", c=4),
                       bg_b[:].unsqueeze(1).to_broadcast([P, 4, EXPERTS]), ALU.add).then_inc(S["logit_done"], 1)
                    after("logit_done")
                    vec.tensor_reduce(top1[:], logits[:], AX.X, ALU.max).then_inc(S["top1_done"], 1)
                if t == 17:
                    after("top1_done")
                    tt(hit1[:], logits[:], per_tile(top1), ALU.is_equal).then_inc(S["hit1_done"], 1)
                    after("hit1_done")
                    tt(sel1[:], hit1[:], rank[:], ALU.mult).then_inc(S["pick1_done"], 1)
                if t == 18:
                    after("pick1_done")
                    vec.tensor_reduce(rank1[:], sel1[:], AX.X, ALU.max).then_inc(S["rank1_done"], 1)
                    after("rank1_done")
                    tt(hit1[:], sel1[:], per_tile(rank1), ALU.is_equal).then_inc(S["sel1_done"], 1)
                if t == 19:
                    after("sel1_done")
                    vec.scalar_tensor_tensor(out=rest[:], in0=hit1[:], scalar=-3.0e38, in1=logits[:],
                                             op0=ALU.mult, op1=ALU.add).then_inc(S["rest_done"], 1)
                    after("rest_done")
                    vec.tensor_reduce(top2[:], rest[:], AX.X, ALU.max).then_inc(S["top2_done"], 1)
                if t == 20:
                    after("top2_done")
                    tt(gap[:], top2[:], top1[:], ALU.subtract).then_inc(S["gap_done"], 1)
                    tt(hit2[:], rest[:], per_tile(top2), ALU.is_equal).then_inc(S["hit2_done"], 1)
                    after("hit2_done")
                    tt(sel2[:], hit2[:], rank[:], ALU.mult).then_inc(S["pick2_done"], 1)
                if t == 21:
                    after("pick2_done")
                    vec.tensor_reduce(rank2[:], sel2[:], AX.X, ALU.max).then_inc(S["rank2_done"], 1)
                    after("rank2_done")
                    tt(hit2[:], sel2[:], per_tile(rank2), ALU.is_equal).then_inc(S["sel2_done"], 1)
                if t == 22:
                    after("gexp_done")
                    ts(gate_sum[:], gap_exp[:], 1.0, None, ALU.add).then_inc(S["gsum_done"], 1)
                    after("gsum_done")
                    vec.reciprocal(gate1[:], gate_sum[:]).then_inc(S["gate1_done"], 1)
                if t == 23:
                    after("gate1_done")
                    tt(gate2[:], gate1[:], gap_exp[:], ALU.mult).then_inc(S["gate2_done"], 1)
                    tt(sel1[:], hit1[:], per_tile(gate1), ALU.mult).then_inc(S["mix1_done"], 1)
                if t == 24:
                    after("gate2_done")
                    after("sel2_done")
                    tt(sel2[:], hit2[:], per_tile(gate2), ALU.mult).then_inc(S["mix2_done"], 1)
                    after("mix1_done")
                    after("mix2_done")
                    tt(comb[:], sel1[:], sel2[:], ALU.add).then_inc(S["comb_done"], 1)
                if t == 26:
                    after("comb_ps")
                    vec.tensor_copy(comb_t, ps_u[0:EXPERTS, :]).then_inc(S["comb_t_done"], 1)
                    after("comb_t_done")
                    vec.tensor_copy(comb3[0:EXPERTS, :], comb_t).then_inc(S["comb1_done"], 1)
                if t == 27:
                    after("comb1_done")
                    wait(dve, w_done, 3 * EXPERTS)
                    tt(comb_r, comb_t, comb3[0:EXPERTS, :], ALU.subtract).then_inc(S["comb_r_done"], 1)
                    after("comb_r_done")
                    vec.tensor_copy(comb_m, comb_r).then_inc(S["comb2_done"], 1)
                if t == 28:
                    after("comb2_done")
                    vec.tensor_copy(comb3[32:32 + EXPERTS, :], comb_m).then_inc(S["comb3_done"], 1)
                    tt(comb3[64:64 + EXPERTS, :], comb_r, comb_m, ALU.subtract).then_inc(S["comb3_done"], 1)
                n = (t - FIRST - 2) // 3
                if 0 <= n < FT and (t - FIRST) % 3 == 2:
                    after("gate_done", FT, n + 1)
                    vec.scalar_tensor_tensor(out=hid[:, n % 2, :], in0=hid[:, n % 2, :], scalar=1.0,
                                             in1=gate[:, n % 2, :], op0=ALU.add, op1=ALU.mult
                                             ).then_inc(S["silu_done"], 1)
                n = (t - FIRST - 3) // 3
                if 0 <= n < FT and (t - FIRST) % 3 == 0:
                    after("up_ps", FT, n + 1)
                    after("silu_done", FT, n + 1)
                    vec.scalar_tensor_tensor(out=hid[:, n % 2, :], in0=ps_u[:], scalar=b0_c[:, n:n + 1],
                                             in1=hid[:, n % 2, :], op0=ALU.add, op1=ALU.mult
                                             ).then_inc(S["hid_done"], 1)
                e = (t - FIRST - 18) // 12
                if 0 <= e < EXPERTS and (t - FIRST - 18) % 12 == 0:
                    after("y_ps", FT, HC * (e + 1))
                    after("y_done", EXPERTS, e)
                    tt(y_scaled, ps_y[:], comb_b[:, e, :], ALU.mult).then_inc(S["y_scaled_done"], 1)
                if t == STEPS + 11:
                    after("final_ps")
                    after("base_done")
                    tt(out_sb[:], ps_y[:].rearrange("p (c d) -> p c d", c=4), out_sb[:],
                       ALU.add).then_inc(S["out_done"], 1)

            def body(pair, attention, experts, tail):
                for s in range(STEPS):
                    if experts and s == 9:
                        wait(dve, S["st_done"], pair(1, 0))
                    if attention and has_max(pair, s):
                        m = s + AHEAD
                        max_step(pair, m)
                        for step in range(4):
                            if m % HSTEPS == (HSTEPS - 1 + step) % HSTEPS:
                                row_maxima(pair, (m - step) // HSTEPS, step)
                    if tail:
                        expert_steps(pair, s + STEPS, 2)
                    if experts:
                        expert_steps(pair, s, 1)
                    if attention and not has_max(pair, s) and has_max(pair, s - 3):
                        for step in range(1, 4):
                            if (s + AHEAD - step) % HSTEPS == HSTEPS - 1:
                                row_maxima(pair, (s + AHEAD - step) // HSTEPS, step)

            nc.vector.memset(k_exp[ROWS:ROWS + 3, :, :], 1.0).then_inc(ones_done, 1)
            nc.vector.memset(rowmax[:, KEYB:], 0.0).then_inc(ones_done, 1)
            dve.wait_ge(ones_done, 2)
            start = Pair(dve, 0)
            for s in range(AHEAD):
                max_step(start, s)
                for step in range(4):
                    if s == HSTEPS - 1 + step:
                        row_maxima(start, 0, step)
            over_pairs(dve, body)

        @block.gpsimd
        def _(pool):
            def expert_steps(f, t, back):
                def at(each, more):
                    return f(each, more - back * each)

                if t == 11:
                    wait(pool, S["ve_done"], at(1, 1))
                    nc.gpsimd.tensor_tensor(rstd[:], ve[:], exponent[:, 0:4], ALU.pow).then_inc(S["rs_done"], 1)
                n = (t - FIRST - 4) // 3
                if 0 <= n < FT and (t - FIRST) % 3 == 2:
                    wait(pool, S["hi_done"], at(FT, n + 1))
                    nc.gpsimd.tensor_tensor(hid_l[:, n % 2, :], hid[:, n % 2, :], hid_h[:, n % 2, :].bitcast(F32),
                                            ALU.subtract).then_inc(S["lo_done"], 1)
                e = (t - FIRST - 18) // 12
                if 0 <= e < EXPERTS and (t - FIRST - 18) % 12 == 0:
                    wait(pool, S["y_scaled_done"], at(EXPERTS, e + 1))
                    wait(pool, S["y_done"], at(EXPERTS, e))
                    if e == 0:
                        wait(pool, S["y_init"], at(1, 1))
                    nc.gpsimd.tensor_tensor(y_sum, y_sum, y_scaled, ALU.add).then_inc(S["y_done"], 1)

            def body(pair, attention, experts, tail):
                for s in range(STEPS):
                    if tail:
                        expert_steps(pair, s + STEPS, 2)
                    if experts:
                        expert_steps(pair, s, 1)

            def load(i):
                w, e = i // EXPERTS, i % EXPERTS
                if i >= 2:
                    pool.wait_ge(w_done, i - 1)
                src = (W0[e], W1[e], W2[e].rearrange("(c p) d -> p c d", p=P))[w]
                dst = w_raw[:, i % 2, :]
                if w == 2:
                    dst = dst.rearrange("p (c d) -> p c d", c=HC)
                pool.dma_start(dst, src).then_inc(w_landed[i % 2], 16)

            load(0)
            for i in range(3 * EXPERTS):
                if i + 1 < 3 * EXPERTS:
                    load(i + 1)
                w, e = i // EXPERTS, i % EXPERTS
                pool.wait_ge(w_landed[i % 2], 16 * (i // 2 + 1))
                nc.gpsimd.tensor_scalar(w_h[w][:, e, :], w_raw[:, i % 2, :], 1.0, 0.0, ALU.mult,
                                        ALU.add).then_inc(wh_done, 1)
                pool.wait_ge(wh_done, i + 1)
                nc.gpsimd.tensor_tensor(w_l[w][:, e, :], w_raw[:, i % 2, :], w_h[w][:, e, :].bitcast(F32),
                                        ALU.subtract).then_inc(w_done, 1)
            over_pairs(pool, body)


def block_kernel(nc, x, Wq, bq, Wk, bk, Wv, bv, gamma, beta, Wg, bg, W0, b0, W1, b1, W2, b2, out):
    parts_d = nc.dram_tensor("parts_scratch", [2, 3, BATCH, P, SEQ], BF16).ap()
    values_d = nc.dram_tensor("values_scratch", [BATCH, HEADS, P, KEYB * VW], F32).ap()
    with ExitStack() as ctx:
        def sb(name, shape, dt=F32):
            return ctx.enter_context(nc.sbuf_tensor(name, shape, dt))

        keep = (sb("ident", [P, P]), sb("rank", [P, 4, EXPERTS]), sb("bg_b", [P, EXPERTS]),
                sb("wg_h", [P, EXPERTS], F32R), sb("wg_l", [P, EXPERTS], F32R),
                sb("b0_c", [P, FT]), sb("b1_c", [P, FT]), sb("b1h_c", [P, FT]),
                sb("b2_sb", [EXPERTS, D]), sb("sel", [96, EXPERTS, P], BF16), sb("comb3", [96, 512], BF16),
                sb("exponent", [P, 4]))
        setup_stage(nc, (x, Wq, bq, Wk, bk, Wv, bv, gamma, beta, Wg, bg, b0, b1, b2), (parts_d, values_d), keep)
        main_stage(nc, x, (W0, W1, W2), out, (parts_d, values_d), keep)


_INS = ["L0_attn_x", "L0_attn_Wq", "L0_attn_bq", "L0_attn_Wk", "L0_attn_bk", "L0_attn_Wv", "L0_attn_bv",
        "L0_attn_gamma", "L0_attn_beta", "L0_ffn_Wg", "L0_ffn_bg", "L0_ffn_W0", "L0_ffn_b0", "L0_ffn_W1",
        "L0_ffn_b1", "L0_ffn_W2", "L0_ffn_b2"]


def kernel(**inputs):
    import numpy as _np
    import concourse.bacc as _bacc
    from concourse import mybir as _mybir
    from concourse.bass_utils import run_bass_kernel_spmd as _run

    nc = _bacc.Bacc("TRN2", target_bir_lowering=False, num_devices=1)
    arrays, args = {}, []
    for name in _INS:
        a = _np.ascontiguousarray(inputs[name])
        arrays[f"in_{name}_dram"] = a
        args.append(nc.dram_tensor(f"in_{name}_dram", a.shape, _mybir.dt.from_np(a.dtype), kind="ExternalInput").ap())
    out = nc.dram_tensor("out_dram", (BATCH, SEQ, D), F32, kind="ExternalOutput").ap()
    block_kernel(nc, *args, out)
    r = _run(nc, [arrays], core_ids=[0])
    return r.results[0]["out_dram"]
```

```python
from contextlib import ExitStack

import concourse.bass as bass
from concourse import mybir

ALU = mybir.AluOpType
ACT = mybir.ActivationFunctionType
AX = mybir.AxisListType
F32 = mybir.dt.float32
F32R = mybir.dt.float32r
BF16 = mybir.dt.bfloat16

P = 128
BATCH, SEQ, D = 2, 2048, 128
HEADS, DK = 8, 16
EXPERTS, HID = 8, 512
EPS = 1e-5
TOKENS = BATCH * SEQ
TILES = TOKENS // P
GROUPS = TILES // 4
NHEADS = BATCH * HEADS
PAIRS = NHEADS // 2
KEYB = SEQ // P
QC = SEQ // 512
STEPS = 2 * KEYB * QC
HSTEPS = STEPS // 2
VW = 32
PRODUCTS = ((0, 0), (0, 1), (0, 2), (1, 0), (1, 1), (2, 0))
ROWS = DK * len(PRODUCTS)
LEAD = 3
AHEAD = (KEYB + LEAD) * QC
HC = HID // P
FT = EXPERTS * HC
PER_TILE = STEPS // FT
FIRST = 40
STACK_SEM = 16 * 2 * len(PRODUCTS)
MROW_SEM = 16 * 3 * 4


def wait(eng, sem, n):
    if isinstance(n, tuple):
        base, more, level = n
        if more:
            eng.reg_add(level, base, more)
        eng.wait_ge(sem, level if more else base)
    elif n > 0:
        eng.wait_ge(sem, n)


class Pair:

    def __init__(self, eng, p, bases=None):
        self.eng, self.p, self.bases = eng, p, bases

    def __call__(self, each, more):
        if isinstance(self.p, int):
            return self.p * each + more
        return self.bases[each], more, self.bases["level"]

    def number(self, each, more):
        return self.p * each + more


RATES = sorted({1, 2, 3, 4, 8, 16, 32, STEPS, STACK_SEM, MROW_SEM})


def over_pairs(eng, body):
    body(Pair(eng, 0), True, False, False)
    body(Pair(eng, 1), True, True, False)
    bases = {each: eng.alloc_register(f"pairs_times_{each}") for each in RATES}
    bases["level"] = eng.alloc_register("level")
    with eng.Fori(2, PAIRS - 1) as p:
        for each in RATES:
            eng.reg_mov(bases[each], p * each)
        body(Pair(eng, p, bases), True, True, True)
    body(Pair(eng, PAIRS - 1), True, True, True)
    body(Pair(eng, PAIRS), False, True, True)
    body(Pair(eng, PAIRS + 1), False, False, True)


def has_max(pair, s):
    return not isinstance(pair.p, int) or 2 * pair.p + (s + AHEAD) // HSTEPS < NHEADS


def setup_stage(nc, io, scratch, keep):
    (x, Wq, bq, Wk, bk, Wv, bv, gamma, beta, Wg, bg, b0, b1, b2) = io
    parts_d, values_d = scratch
    (ident, rank, bg_b, wg_h, wg_l, b0_c, b1_c, b1h_c, b2_sb, sel, comb3, exponent) = keep
    with ExitStack() as ctx:
        def sb(name, shape, dt=F32):
            return ctx.enter_context(nc.sbuf_tensor(name, shape, dt))

        def sem(name):
            return ctx.enter_context(nc.semaphore(name))

        xs = sb("xs", [P, TILES, D])
        xt = sb("xt", [P, TOKENS])
        wq, wk = sb("wq", [P, D]), sb("wk", [P, D])
        wv = sb("wv", [P, HEADS * D])
        wv_sum = sb("wv_sum", [P, D])
        bv_b = sb("bv_b", [P, HEADS * D])
        bv_sum = sb("bv_sum", [P, D])
        gamma_c, beta_c = sb("gamma_c", [P, 1]), sb("beta_c", [P, 1])
        bq_c, bk_c = sb("bq_c", [P, 1]), sb("bk_c", [P, 1])
        wg = sb("wg", [P, EXPERTS])
        b_rows = sb("b_rows", [FT, 2, P])
        stats = sb("stats", [P, TILES, 6])
        mv = sb("mv", [P, TILES, 2])
        ve = sb("ve", [P, TILES])
        rstd = sb("rstd", [P, TILES])
        part = [[sb(f"part{w}{i}", [P, BATCH, SEQ], BF16) for i in range(3)] for w in "qk"]
        qf, kf = sb("qf", [P, 2, 512]), sb("kf", [P, 2, 512])
        qr, kr = sb("qr", [P, 2, 512]), sb("kr", [P, 2, 512])
        vh = sb("vh", [P, BATCH, HEADS, KEYB, VW])
        ps_t, ps_q, ps_k, ps_v = [
            [ctx.enter_context(nc.psum_tensor(f"ps_{n}{i}", [P, 512], F32)) for i in range(2)]
            for n in "tqkv"]

        x_landed = [sem(f"x_landed{g}") for g in range(GROUPS)]
        qkw_landed, wv_landed, cols_landed = sem("qkw_landed"), sem("wv_landed"), sem("cols_landed")
        keep_landed = sem("keep_landed")
        sums_done, stats_done, mv_done, ve_done = sem("sums_done"), sem("stats_done"), sem("mv_done"), sem("ve_done")
        rstd_done, xhat_done, tr_done, xt_done = sem("rstd_done"), sem("xhat_done"), sem("tr_done"), sem("xt_done")
        q_ps, k_ps, v_ps = sem("q_ps"), sem("k_ps"), sem("v_ps")
        qf_done, q1_done, qr_done, q2_done, q3_done = [sem(f"{n}_done") for n in ("qf", "q1", "qr", "q2", "q3")]
        kf_done, k1_done, kr_done, k2_done, k3_done = [sem(f"{n}_done") for n in ("kf", "k1", "kr", "k2", "k3")]
        v_done, vh_zero, vh_one, ident_zero, ident_done, const_zero, const_done = [
            sem(n) for n in ("v_done", "vh_zero", "vh_one", "ident_zero", "ident_done", "const_zero", "const_done")]
        wgh_done, wgl_done, b_cols, b1h_done, scratch_written = [
            sem(n) for n in ("wgh_done", "wgl_done", "b_cols", "b1h_done", "scratch_written")]

        x_t = x.rearrange("b (n p) d -> p (b n) d", p=P)

        def col(v):
            return v.rearrange("(p a) -> p a", a=1)

        with nc.Block() as block:
            @block.sync
            def _(sp):
                for g in range(GROUPS):
                    sp.dma_start(xs[:, 4 * g:4 * g + 4, :], x_t[:, 4 * g:4 * g + 4, :]).then_inc(x_landed[g], 16)
                for b in range(BATCH):
                    done = GROUPS // BATCH * (b + 1)
                    for i, (sq, sk) in enumerate(((q1_done, k1_done), (q2_done, k2_done), (q3_done, k3_done))):
                        sp.wait_ge(sq, done)
                        sp.dma_start(parts_d[0, i, b], part[0][i][:, b, :]).then_inc(scratch_written, 16)
                        sp.wait_ge(sk, done)
                        sp.dma_start(parts_d[1, i, b], part[1][i][:, b, :]).then_inc(scratch_written, 16)
                    sp.wait_ge(v_done, done)
                    sp.dma_start(values_d[b].rearrange("h p v -> p h v"),
                                 vh[:, b].rearrange("p h k v -> p h (k v)")).then_inc(scratch_written, 16)
                sp.wait_ge(scratch_written, 16 * 7 * BATCH)
                sp.wait_ge(keep_landed, 16 * 4)

            @block.gpsimd
            def _(pool):
                nc.gpsimd.memset(ident[:], 0.0).then_inc(ident_zero, 1)
                pool.wait_ge(ident_zero, 1)
                nc.gpsimd.affine_select(out=ident[:], in_=ident[:], compare_op=ALU.not_equal, fill=1.0, base=0,
                                        pattern=[[-1, P]], channel_multiplier=1).then_inc(ident_done, 1)
                nc.gpsimd.memset(exponent[:], -0.5).then_inc(const_done, 1)
                nc.gpsimd.memset(vh[:, :, :, :, DK + 1:VW], 0.0).then_inc(vh_one, 1)
                nc.gpsimd.memset(vh[:, :, :, :, DK:DK + 1], 1.0).then_inc(vh_one, 1)
                pool.wait_ge(const_done, 1)

                def rsqrt(g):
                    pool.wait_ge(ve_done, g + 1)
                    nc.gpsimd.tensor_tensor(rstd[:, 4 * g:4 * g + 4], ve[:, 4 * g:4 * g + 4],
                                            exponent[:, 0:4], ALU.pow).then_inc(rstd_done, 1)

                rsqrt(0)
                for g in range(GROUPS):
                    if g + 1 < GROUPS:
                        rsqrt(g + 1)
                    b, c = g // 4, 512 * (g % 4)
                    pool.wait_ge(k1_done, g + 1)
                    nc.gpsimd.tensor_tensor(kr[:, g % 2, :], kf[:, g % 2, :], part[1][0][:, b, c:c + 512],
                                            ALU.subtract).then_inc(kr_done, 1)
                    pool.wait_ge(k2_done, g + 1)
                    nc.gpsimd.tensor_tensor(part[1][2][:, b, c:c + 512], kr[:, g % 2, :],
                                            part[1][1][:, b, c:c + 512], ALU.subtract).then_inc(k3_done, 1)
                nc.gpsimd.memset(sel[:], 0.0).then_inc(const_zero, 1)
                nc.gpsimd.memset(comb3[:], 0.0)
                for e in range(EXPERTS):
                    nc.gpsimd.memset(rank[:, :, e:e + 1], float(EXPERTS - e))
                for part_no in range(3):
                    pool.wait_ge(const_zero, part_no + 1)
                    nc.gpsimd.affine_select(out=sel[:], in_=sel[:], compare_op=ALU.not_equal, fill=1.0,
                                            base=-32 * part_no, pattern=[[-1, EXPERTS], [0, P]],
                                            channel_multiplier=1).then_inc(const_zero, 1)
                pool.wait_ge(const_zero, 4)

            @block.scalar
            def _(act):
                act.dma_start(wq[:], Wq).then_inc(qkw_landed, 16)
                act.dma_start(wk[:], Wk).then_inc(qkw_landed, 16)
                for dst, src in ((gamma_c, gamma), (beta_c, beta), (bq_c, bq), (bk_c, bk)):
                    act.dma_start(dst[:], col(src)).then_inc(cols_landed, 16)
                act.dma_start(wg[:], Wg).then_inc(cols_landed, 16)
                act.dma_start(wv[:], Wv).then_inc(wv_landed, 16)
                act.dma_start(bv_b[:], bv.partition_broadcast(P)).then_inc(wv_landed, 16)
                act.dma_start(bg_b[:], bg.partition_broadcast(P)).then_inc(keep_landed, 16)
                act.dma_start(b_rows[:, 0, :], b0.rearrange("e (c p) -> (e c) p", p=P)).then_inc(keep_landed, 16)
                act.dma_start(b_rows[:, 1, :], b1.rearrange("e (c p) -> (e c) p", p=P)).then_inc(keep_landed, 16)
                act.dma_start(b2_sb[:], b2).then_inc(keep_landed, 16)
                act.wait_ge(cols_landed, 16 * 5)

                def norm_out(g):
                    act.wait_ge(tr_done, g + 1)
                    nc.scalar.activation(xt[:, 512 * g:512 * g + 512], ps_t[g % 2][:], ACT.Identity,
                                         bias=beta_c[:], scale=gamma_c[:]).then_inc(xt_done, 1)

                norm_out(0)
                for g in range(GROUPS):
                    if g + 1 < GROUPS:
                        norm_out(g + 1)
                    b, c = g // 4, 512 * (g % 4)
                    act.wait_ge(k_ps, g + 1)
                    if g >= 2:
                        act.wait_ge(kr_done, g - 1)
                    nc.scalar.activation(kf[:, g % 2, :], ps_k[g % 2][:], ACT.Identity,
                                         bias=bk_c[:]).then_inc(kf_done, 1)
                    act.wait_ge(qf_done, g + 1)
                    nc.scalar.activation(part[0][0][:, b, c:c + 512], qf[:, g % 2, :], ACT.Copy).then_inc(q1_done, 1)
                    act.wait_ge(kf_done, g + 1)
                    nc.scalar.activation(part[1][0][:, b, c:c + 512], kf[:, g % 2, :], ACT.Copy).then_inc(k1_done, 1)
                    act.wait_ge(qr_done, g + 1)
                    nc.scalar.activation(part[0][1][:, b, c:c + 512], qr[:, g % 2, :], ACT.Copy).then_inc(q2_done, 1)
                    act.wait_ge(kr_done, g + 1)
                    nc.scalar.activation(part[1][1][:, b, c:c + 512], kr[:, g % 2, :], ACT.Copy).then_inc(k2_done, 1)
                act.wait_ge(b_cols, 1)
                nc.scalar.activation(b0_c[:], ps_t[0][:, 0:FT], ACT.Copy)
                nc.scalar.activation(b1_c[:], ps_t[0][:, FT:2 * FT], ACT.Copy)
                nc.scalar.mul(b1h_c[:], ps_t[0][:, FT:2 * FT], 0.5).then_inc(b1h_done, 1)

            @block.vector
            def _(dve):
                def moments(g):
                    dve.wait_ge(x_landed[g], 16)
                    for j in range(4 * g, 4 * g + 4):
                        last = nc.vector.bn_stats(stats[:, j, :], xs[:, j, :])
                    last.then_inc(stats_done, 1)
                    dve.wait_ge(stats_done, g + 1)
                    for j in range(4 * g, 4 * g + 4):
                        last = nc.vector.bn_aggr(mv[:, j, :], stats[:, j, :])
                    last.then_inc(mv_done, 1)
                    dve.wait_ge(mv_done, g + 1)
                    nc.vector.tensor_scalar(ve[:, 4 * g:4 * g + 4], mv[:, 4 * g:4 * g + 4, 1], 1.0 + EPS, EPS * EPS,
                                            ALU.mult, ALU.add).then_inc(ve_done, 1)

                def normalise(g):
                    dve.wait_ge(rstd_done, g + 1)
                    for j in range(4 * g, 4 * g + 4):
                        last = nc.vector.tensor_scalar(xs[:, j, :], xs[:, j, :], mv[:, j, 0:1], rstd[:, j:j + 1],
                                                       ALU.subtract, ALU.mult)
                    last.then_inc(xhat_done, 1)

                def queries_and_values(g):
                    b, c = g // 4, 512 * (g % 4)
                    dve.wait_ge(q_ps, g + 1)
                    if g >= 2:
                        dve.wait_ge(q1_done, g - 1)
                        dve.wait_ge(qr_done, g - 1)
                    nc.vector.tensor_scalar(qf[:, g % 2, :], ps_q[g % 2][:], bq_c[:], float(DK) ** -0.5,
                                            ALU.add, ALU.mult).then_inc(qf_done, 1)
                    dve.wait_ge(v_ps, g + 1)
                    for j in range(4):
                        last = nc.vector.tensor_tensor(
                            vh[:, b, :, 4 * (g % 4) + j, 0:DK],
                            ps_v[g % 2][:, D * j:D * j + D].rearrange("p (h v) -> p h v", v=DK),
                            bv_sum[:].rearrange("p (h v) -> p h v", v=DK), ALU.add)
                    last.then_inc(v_done, 1)
                    dve.wait_ge(q1_done, g + 1)
                    if g >= 2:
                        dve.wait_ge(q2_done, g - 1)
                        dve.wait_ge(q3_done, g - 1)
                    nc.vector.tensor_tensor(qr[:, g % 2, :], qf[:, g % 2, :], part[0][0][:, b, c:c + 512],
                                            ALU.subtract).then_inc(qr_done, 1)
                    dve.wait_ge(q2_done, g + 1)
                    dve.wait_ge(qr_done, g + 1)
                    nc.vector.tensor_tensor(part[0][2][:, b, c:c + 512], qr[:, g % 2, :],
                                            part[0][1][:, b, c:c + 512], ALU.subtract).then_inc(q3_done, 1)

                moments(0)
                dve.wait_ge(wv_landed, 32)
                nc.vector.tensor_reduce(wv_sum[:], wv[:].rearrange("p (j n) -> p j n", n=HEADS), AX.X,
                                        ALU.add).then_inc(sums_done, 1)
                nc.vector.tensor_reduce(bv_sum[:], bv_b[:].rearrange("p (j n) -> p j n", n=HEADS), AX.X,
                                        ALU.add).then_inc(sums_done, 1)
                dve.wait_ge(cols_landed, 16 * 5)
                nc.vector.tensor_copy(wg_h[:], wg[:]).then_inc(wgh_done, 1)
                moments(1)
                normalise(0)
                dve.wait_ge(sums_done, 2)
                dve.wait_ge(vh_one, 2)
                for g in range(GROUPS):
                    if g + 2 < GROUPS:
                        moments(g + 2)
                    if g + 1 < GROUPS:
                        normalise(g + 1)
                    queries_and_values(g)
                dve.wait_ge(wgh_done, 1)
                nc.vector.tensor_tensor(wg_l[:], wg[:], wg_h[:].bitcast(F32), ALU.subtract).then_inc(wgl_done, 1)
                dve.wait_ge(wgl_done, 1)

            @block.tensor
            def _(pe):
                def transposes(g):
                    pe.wait_ge(xhat_done, g + 1)
                    if g >= 2:
                        pe.wait_ge(xt_done, g - 1)
                    for j in range(4):
                        last = nc.tensor.transpose(ps_t[g % 2][:, P * j:P * j + P], xs[:, 4 * g + j, :], ident[:])
                    last.then_inc(tr_done, 1)

                pe.wait_ge(ident_done, 1)
                transposes(0)
                pe.wait_ge(qkw_landed, 32)
                pe.wait_ge(sums_done, 1)
                for g in range(GROUPS):
                    if g + 1 < GROUPS:
                        transposes(g + 1)
                    pe.wait_ge(xt_done, g + 1)
                    if g >= 2:
                        pe.wait_ge(kf_done, g - 1)
                    nc.tensor.matmul(ps_k[g % 2][:], wk[:], xt[:, 512 * g:512 * g + 512], start=True,
                                     stop=True).then_inc(k_ps, 1)
                    if g >= 2:
                        pe.wait_ge(qf_done, g - 1)
                    nc.tensor.matmul(ps_q[g % 2][:], wq[:], xt[:, 512 * g:512 * g + 512], start=True,
                                     stop=True).then_inc(q_ps, 1)
                    if g >= 2:
                        pe.wait_ge(v_done, g - 1)
                    for j in range(4):
                        last = nc.tensor.matmul(ps_v[g % 2][:, P * j:P * j + P],
                                                xt[:, 512 * g + P * j:512 * g + P * j + P], wv_sum[:],
                                                start=True, stop=True)
                    last.then_inc(v_ps, 1)
                pe.wait_ge(keep_landed, 16 * 4)
                for i in range(2):
                    last = nc.tensor.transpose(ps_t[0][:, FT * i:FT * i + FT], b_rows[:, i, :], ident[0:FT, 0:FT])
                last.then_inc(b_cols, 1)


def main_stage(nc, x, weights, out, scratch, keep):
    parts_d, values_d = scratch
    (ident, rank, bg_b, wg_h, wg_l, b0_c, b1_c, b1h_c, b2_sb, sel, comb3, exponent) = keep
    W0, W1, W2 = weights
    with ExitStack() as ctx:
        def sb(name, shape, dt=F32):
            return ctx.enter_context(nc.sbuf_tensor(name, shape, dt))

        def sem(name):
            return ctx.enter_context(nc.semaphore(name))

        w_h = [sb(f"w{i}_h", [P, EXPERTS, 512], F32R) for i in range(3)]
        w_l = [sb(f"w{i}_l", [P, EXPERTS, 512], F32R) for i in range(3)]
        w_raw = sb("w_raw", [P, 2, 512])
        q_max, k_max = sb("q_max", [P, 2, SEQ], BF16), sb("k_max", [P, 2, SEQ], BF16)
        q_exp, k_exp = sb("q_exp", [P, 2, SEQ], BF16), sb("k_exp", [P, 2, SEQ], BF16)
        values = sb("values", [P, 2, KEYB, VW])
        blockmax = sb("blockmax", [P, 2, KEYB, QC])
        rowmax = sb("rowmax", [P, 32])
        rowmax_t = sb("rowmax_t", [P, 32])
        negmax = sb("negmax", [P, 32])
        negmax_r = sb("negmax_r", [P, 32])
        m_parts = sb("m_parts", [P, 2, 3, 32], BF16)
        probs = sb("probs", [P, 2, QC, 512])
        o_sb = sb("o_sb", [P, 2, 512])
        x_in = sb("x_in", [P, 4, D])
        x_res = sb("x_res", [P, 4, D])
        x_hat = sb("x_hat", [P, 4, D])
        inv_den = sb("inv_den", [P, 8, 4])
        stats = sb("stats2", [P, 4, 6])
        mv = sb("mv2", [P, 4, 2])
        ve = sb("ve2", [P, 4])
        rstd = sb("rstd2", [P, 4])
        next_h, next_l = sb("next_h", [P, 512], F32R), sb("next_l", [P, 512], F32R)
        xt_h, xt_l = sb("xt_h", [P, 512], F32R), sb("xt_l", [P, 512], F32R)
        logits = sb("logits", [P, 4, EXPERTS])
        top1, top2, rank1, rank2 = [sb(n, [P, 4]) for n in ("top1", "top2", "rank1", "rank2")]
        hit1, hit2, sel1, sel2, rest = [sb(n, [P, 4, EXPERTS]) for n in ("hit1", "hit2", "sel1", "sel2", "rest")]
        gap, gap_exp, gate_sum, gate1, gate2 = [sb(n, [P, 4]) for n in ("gap", "gap_exp", "gate_sum", "gate1", "gate2")]
        comb = sb("comb", [P, 4, EXPERTS])
        comb_t = x_in[0:EXPERTS].rearrange("p c d -> p (c d)")
        comb_m, comb_r = sb("comb_m", [EXPERTS, 512], BF16), sb("comb_r", [EXPERTS, 512])
        comb_b = sb("comb_b", [P, 2, 512])
        hid, gate = sb("hid", [P, 2, 512]), sb("gate", [P, 2, 512])
        hid_h, hid_l = sb("hid_h", [P, 2, 512], F32R), sb("hid_l", [P, 2, 512], F32R)
        y_sum, y_scaled = w_raw[:, 0, :], w_raw[:, 1, :]
        out_sb = sb("out_sb", [P, 4, D])

        ps_s = [ctx.enter_context(nc.psum_tensor(f"ps_s{i}", [P, 512], F32)) for i in range(2)]
        ps_m = [ctx.enter_context(nc.psum_tensor(f"ps_m{i}", [P, 512], F32)) for i in range(2)]
        ps_o, ps_g, ps_u, ps_y = [ctx.enter_context(nc.psum_tensor(n, [P, 512], F32))
                                  for n in ("ps_o", "ps_g", "ps_u", "ps_y")]

        max_landed = [sem(f"max_landed{i}") for i in range(2)]
        exp_landed = [sem(f"exp_landed{i}") for i in range(2)]
        values_landed = [sem(f"values_landed{i}") for i in range(2)]
        mrow_landed = [sem(f"mrow_landed{i}") for i in range(2)]
        ones_done, max_ps, max_done = sem("ones_done"), sem("max_ps"), sem("max_done")
        fold_done, fold_t, neg_done, m1_done, negr_done, m2_done, m_ready = [
            sem(n) for n in ("fold_done", "fold_t", "neg_done", "m1_done", "negr_done", "m2_done", "m_ready")]
        score_ps, probs_done, pv_done, o_done = sem("score_ps"), sem("probs_done"), sem("pv_done"), sem("o_done")
        w_landed = [sem(f"w_landed{i}") for i in range(2)]
        wh_done, w_done = sem("wh_done"), sem("w_done")
        names = ("xin_landed o_turned den_done att_done xres_done st_done mv_done ve_done rs_done xhat_done xt_ps h_moved l_moved "
                 "xth_done xtl_done logit_ps logit_done top1_done hit1_done pick1_done rank1_done sel1_done "
                 "rest_done top2_done hit2_done pick2_done rank2_done sel2_done gap_done gexp_done gsum_done "
                 "gate1_done gate2_done mix1_done mix2_done comb_done comb_ps comb_t_done comb1_done comb_r_done "
                 "comb2_done comb3_done b2_ps y_init bcast_ps bcast_done gate_ps up_ps gate_done "
                 "silu_done hid_done hi_done lo_done y_ps y_scaled_done y_done final_ps base_done out_done").split()
        S = {n: sem("e_" + n) for n in names}
        out_stored = sem("out_stored")

        x_pairs = x.rearrange("b s d -> (b s) d").rearrange("(f h c q) d -> f h q c d", h=2, c=4, q=64)
        out_pairs = out.rearrange("b s d -> (b s) d").rearrange("(f h c q) d -> f h q c d", h=2, c=4, q=64)
        parts_h = parts_d.rearrange("w i b (h k) s -> w i (b h) k s", k=DK)
        values_h = values_d.rearrange("b h p v -> (b h) p v")

        block = ctx.enter_context(nc.Block())

        @block.sync
        def _(sp):
            def load_stack(q, k, par, head, landed):
                for i, (a, b) in enumerate(PRODUCTS):
                    sp.dma_start(q[DK * i:DK * i + DK, par, :], parts_h[0, a, head]).then_inc(landed[par], 16)
                    sp.dma_start(k[DK * i:DK * i + DK, par, :], parts_h[1, b, head]).then_inc(landed[par], 16)

            def load_for_max(pair, h):
                wait(sp, max_ps, pair(STEPS, HSTEPS * (h - 1)))
                load_stack(q_max, k_max, h % 2, pair.number(2, h), max_landed)

            def load_for_exp(pair, h):
                wait(sp, score_ps, pair(STEPS, HSTEPS * (h - 1)))
                load_stack(q_exp, k_exp, h % 2, pair.number(2, h), exp_landed)
                wait(sp, pv_done, pair(2 * KEYB, KEYB * (h - 1)))
                sp.dma_start(values[:, h % 2].rearrange("p k v -> p (k v)"),
                             values_h[pair.number(2, h)]).then_inc(values_landed[h % 2], 16)

            def load_m_rows(pair, h):
                wait(sp, m_ready, pair(2, h + 1))
                for i in range(3):
                    row = q_exp[ROWS + i:ROWS + i + 1, h % 2, :].rearrange("a (c q s) -> a q c s", q=4, s=32)
                    for q in range(4):
                        sp.dma_start(row[:, q], m_parts[32 * q:32 * q + KEYB, h % 2, i, :]
                                     ).then_inc(mrow_landed[h % 2], 16)

            def body(pair, attention, experts, tail):
                if experts:
                    wait(sp, S["b2_ps"], pair(1, -1))
                    for h in range(2):
                        sp.dma_start(x_in[64 * h:64 * h + 64], x_pairs[pair.number(1, -1), h]
                                     ).then_inc(S["xin_landed"], 16)
                last = isinstance(pair.p, int) and pair.p == PAIRS - 1
                if attention:
                    if not last:
                        load_for_max(pair, 2)
                    load_for_exp(pair, 1)
                    load_m_rows(pair, 1)
                if tail:
                    wait(sp, S["out_done"], pair(1, -1))
                    for h in range(2):
                        sp.dma_start(out_pairs[pair.number(1, -2), h], out_sb[64 * h:64 * h + 64]
                                     ).then_inc(out_stored, 16)
                if attention:
                    if not last:
                        load_for_max(pair, 3)
                        load_for_exp(pair, 2)
                        load_m_rows(pair, 2)

            start = Pair(sp, 0)
            load_for_max(start, 0)
            load_for_max(start, 1)
            load_for_exp(start, 0)
            load_m_rows(start, 0)
            over_pairs(sp, body)
            sp.wait_ge(out_stored, 32 * PAIRS)

        @block.tensor
        def _(pe):
            def max_block(pair, s):
                head, par = s // HSTEPS, s // HSTEPS % 2
                c, j = s % HSTEPS // QC, s % QC
                if s % HSTEPS == 0:
                    wait(pe, max_landed[par], pair(STACK_SEM, STACK_SEM * (head // 2 + 1)))
                wait(pe, max_done, pair(STEPS, s - 1))
                nc.tensor.matmul(ps_m[s % 2][:], q_max[0:ROWS, par, P * c:P * c + P],
                                 k_max[0:ROWS, par, 512 * j:512 * j + 512], start=True,
                                 stop=True).then_inc(max_ps, 1)

            def score_block(pair, s):
                par, t, j = s // HSTEPS, s % HSTEPS // QC, s % QC
                if s % HSTEPS == 0:
                    wait(pe, exp_landed[par], pair(STACK_SEM, STACK_SEM))
                    wait(pe, mrow_landed[par], pair(MROW_SEM, MROW_SEM))
                wait(pe, probs_done, pair(STEPS, s - 1))
                nc.tensor.matmul(ps_s[s % 2][:], k_exp[0:ROWS + 3, par, P * t:P * t + P],
                                 q_exp[0:ROWS + 3, par, 512 * j:512 * j + 512], start=True,
                                 stop=True).then_inc(score_ps, 1)

            def value_products(pair, k):
                par, t = k // KEYB % 2, k % KEYB
                if t == 0:
                    wait(pe, values_landed[par], pair(16, 16))
                    wait(pe, o_done, pair(2, k // KEYB))
                wait(pe, probs_done, pair(STEPS, QC * k + QC))
                for j in range(QC):
                    last = nc.tensor.matmul(ps_o[VW * j:VW * j + VW, :], values[:, par, t, :],
                                            probs[:, k % 2, j, :], start=(t == 0), stop=(t == KEYB - 1),
                                            tile_position=(0, VW * j))
                last.then_inc(pv_done, 1)

            def product(ps, wh, wl, ah, al, start, stop):
                nc.tensor.matmul(ps, wh, ah, start=start, stop=False)
                nc.tensor.matmul(ps, wl, ah, start=False, stop=False)
                return nc.tensor.matmul(ps, wh, al, start=False, stop=stop)

            def tile_products(f, t, back):
                def at(each, more):
                    return f(each, more - back * each)

                n, kind = (t - FIRST) // PER_TILE, (t - FIRST) % PER_TILE
                if 0 <= n < FT and kind == 1:
                    e, c = n // HC, P * (n % HC)
                    if n == 0:
                        wait(pe, S["h_moved"], at(1, 1))
                        wait(pe, S["l_moved"], at(1, 1))
                        if isinstance(f.p, int) and f.p == 1:
                            wait(pe, w_done, 3 * EXPERTS)
                    wait(pe, S["gate_done"], at(FT, n))
                    product(ps_g[:], w_h[1][:, e, c:c + P], w_l[1][:, e, c:c + P], xt_h[:], xt_l[:],
                            True, True).then_inc(S["gate_ps"], 1)
                if 0 <= n < FT and kind == 3:
                    e, c = n // HC, P * (n % HC)
                    reader = {3: ("out_done", at(1, 0)), 4: ("y_init", at(1, 1))}
                    reader.update({HC * i + 1: ("bcast_done", at(EXPERTS, i + 1)) for i in range(EXPERTS)})
                    if not (isinstance(f.p, int) and f.p == PAIRS + 1):
                        reader.update({(STEPS + step - FIRST) // PER_TILE: user for step, user in (
                            (5, ("att_done", at(2, 3))), (9, ("att_done", at(2, 4))), (21, ("xtl_done", at(1, 2))),
                            (25, ("logit_done", at(1, 2))), (37, ("comb_t_done", at(1, 2))))})
                    if n in reader:
                        wait(pe, S[reader[n][0]], reader[n][1])
                    wait(pe, S["hid_done"], at(FT, n))
                    product(ps_u[:], w_h[0][:, e, c:c + P], w_l[0][:, e, c:c + P], xt_h[:], xt_l[:],
                            True, True).then_inc(S["up_ps"], 1)
                m = n - 2
                if 0 <= m < FT and kind == 2:
                    e, c = m // HC, m % HC
                    if c == 0:
                        wait(pe, S["y_scaled_done"], at(EXPERTS, e))
                    wait(pe, S["hi_done"], at(FT, m + 1))
                    wait(pe, S["lo_done"], at(FT, m + 1))
                    product(ps_y[:], w_h[2][:, e, P * c:P * c + P], w_l[2][:, e, P * c:P * c + P],
                            hid_h[:, m % 2, :], hid_l[:, m % 2, :], c == 0, c == HC - 1).then_inc(S["y_ps"], 1)

            def other_products(f, t, back):
                def at(each, more):
                    return f(each, more - back * each)

                def bank_is_free():
                    done = (t - FIRST) // PER_TILE
                    wait(pe, S["hid_done"], at(FT, min(done, FT) if isinstance(f.p, int) and f.p == PAIRS + 1 else done))

                if t in (5, 9):
                    half = (t - 5) // 4
                    bank_is_free()
                    wait(pe, o_done, at(2, 2))
                    if half:
                        wait(pe, S["att_done"], at(2, 1))
                    turned = o_sb[:].rearrange("p h (q a) -> p a h q", a=8)
                    for a in range(4):
                        last = nc.tensor.transpose(ps_u[:, P * a:P * a + P], turned[:, 4 * half + a], ident[:])
                    last.then_inc(S["o_turned"], 1)
                if t == 21:
                    bank_is_free()
                    wait(pe, S["xhat_done"], at(1, 1))
                    for c in range(4):
                        last = nc.tensor.transpose(ps_u[:, P * c:P * c + P], x_hat[:, c, :], ident[:])
                    last.then_inc(S["xt_ps"], 1)
                if t == 25:
                    bank_is_free()
                    wait(pe, S["xth_done"], at(1, 1))
                    wait(pe, S["xtl_done"], at(1, 1))
                    for c in range(4):
                        for i, (a, w) in enumerate(((next_h, wg_h), (next_h, wg_l), (next_l, wg_h), (next_l, wg_l))):
                            last = nc.tensor.matmul(ps_u[:, EXPERTS * c:EXPERTS * c + EXPERTS],
                                                    a[:, P * c:P * c + P], w[:], start=(i == 0), stop=(i == 3))
                    last.then_inc(S["logit_ps"], 1)
                if t == 37:
                    bank_is_free()
                    wait(pe, S["comb_done"], at(1, 1))
                    for c in range(4):
                        last = nc.tensor.transpose(ps_u[0:EXPERTS, P * c:P * c + P], comb[:, c, :], ident[:])
                    last.then_inc(S["comb_ps"], 1)
                e = (t - FIRST - 5) // 16
                if 0 <= e < EXPERTS and (t - FIRST) % 16 == 5:
                    bank_is_free()
                    wait(pe, S["comb3_done"], at(2, 2))
                    nc.tensor.matmul(ps_u[:], sel[:, e, :], comb3[:], start=True, stop=True
                                     ).then_inc(S["bcast_ps"], 1)
                if t == FIRST + 17:
                    bank_is_free()
                    nc.tensor.matmul(ps_u[:], b2_sb[:], comb_t, start=True, stop=True).then_inc(S["b2_ps"], 1)
                if t == FIRST + 13 + STEPS:
                    bank_is_free()
                    wait(pe, S["y_done"], at(EXPERTS, EXPERTS))
                    for c in range(4):
                        last = nc.tensor.transpose(ps_u[:, P * c:P * c + P], y_sum[:, P * c:P * c + P], ident[:])
                    last.then_inc(S["final_ps"], 1)

            def body(pair, attention, experts, tail):
                for s in range(STEPS):
                    if attention:
                        score_block(pair, s)
                        if has_max(pair, s):
                            max_block(pair, s + AHEAD)
                    if s % QC == 0 and (s > 0 and attention or s == 0 and experts):
                        value_products(pair, s // QC - 1)
                    for step in (tile_products, other_products):
                        if tail:
                            step(pair, s + STEPS, 2)
                        if experts:
                            step(pair, s, 1)

            pe.wait_ge(ones_done, 2)
            for s in range(AHEAD):
                max_block(Pair(pe, 0), s)
            over_pairs(pe, body)

        @block.scalar
        def _(act):
            def exponentials(pair, s):
                k, j = s // QC, s % QC
                wait(act, score_ps, pair(STEPS, s + 1))
                if j == 0:
                    wait(act, pv_done, pair(2 * KEYB, k - 1))
                nc.scalar.activation(probs[:, k % 2, j, :], ps_s[s % 2][:], ACT.Exp).then_inc(probs_done, 1)

            def copy_sums(pair, h):
                wait(act, pv_done, pair(2 * KEYB, KEYB * (h + 1)))
                wait(act, S["o_turned"], pair(2, 0 if h == 0 else -2))
                nc.scalar.activation(o_sb[:, h % 2, :], ps_o[:], ACT.Copy).then_inc(o_done, 1)

            def before_exponential(f, t, back):
                def at(each, more):
                    return f(each, more - back * each)

                n, kind = (t - FIRST) // PER_TILE, (t - FIRST) % PER_TILE
                if 0 <= n < FT and kind == 2:
                    wait(act, S["gate_ps"], at(FT, n + 1))
                    wait(act, S["lo_done"], at(FT, n - 1))
                    nc.scalar.activation(hid[:, n % 2, :], ps_g[:], ACT.Tanh, bias=b1h_c[:, n:n + 1], scale=0.5)
                if t == 22:
                    wait(act, S["xt_ps"], at(1, 1))
                    wait(act, S["h_moved"], at(1, 0))
                    nc.scalar.activation(next_h[:], ps_u[:], ACT.Copy).then_inc(S["xth_done"], 1)
                e = (t - FIRST - 6) // 16
                if 0 <= e < EXPERTS and (t - FIRST) % 16 == 6:
                    wait(act, S["bcast_ps"], at(EXPERTS, e + 1))
                    wait(act, S["y_scaled_done"], at(EXPERTS, e - 1))
                    nc.scalar.activation(comb_b[:, e % 2, :], ps_u[:], ACT.Copy, scale=0.5
                                         ).then_inc(S["bcast_done"], 1)
                if t == FIRST + 18:
                    wait(act, S["b2_ps"], at(1, 1))
                    act.wait_ge(w_done, 3 * EXPERTS)
                    nc.scalar.activation(y_sum, ps_u[:], ACT.Copy).then_inc(S["y_init"], 1)

            def after_exponential(f, t, back):
                def at(each, more):
                    return f(each, more - back * each)

                n, kind = (t - FIRST) // PER_TILE, (t - FIRST) % PER_TILE
                if 0 <= n < FT and kind == 3:
                    wait(act, S["silu_done"], at(FT, n - 1))
                    nc.scalar.activation(gate[:, n % 2, :], ps_g[:], ACT.Identity, bias=b1_c[:, n:n + 1]
                                         ).then_inc(S["gate_done"], 1)
                n -= 1
                if 0 <= n < FT and kind == 1:
                    wait(act, S["hid_done"], at(FT, n + 1))
                    wait(act, S["y_ps"], at(FT, n - 1))
                    nc.scalar.activation(hid_h[:, n % 2, :], hid[:, n % 2, :], ACT.Copy).then_inc(S["hi_done"], 1)
                if t == 31:
                    wait(act, S["gap_done"], at(1, 1))
                    nc.scalar.activation(gap_exp[:], gap[:], ACT.Exp).then_inc(S["gexp_done"], 1)
                if t == FIRST:
                    wait(act, S["up_ps"], at(FT, 0))
                    wait(act, S["xtl_done"], at(1, 1))
                    nc.scalar.activation(xt_l[:], next_l[:], ACT.Copy).then_inc(S["l_moved"], 1)
                if t == 100:
                    wait(act, S["xres_done"], at(1, 1))
                    wait(act, out_stored, at(32, 0))
                    nc.scalar.activation(out_sb[:], x_res[:], ACT.Copy).then_inc(S["base_done"], 1)

            def body(pair, attention, experts, tail):
                for s in range(STEPS):
                    if tail:
                        before_exponential(pair, s + STEPS, 2)
                    if experts:
                        before_exponential(pair, s, 1)
                    if attention:
                        exponentials(pair, s)
                    if tail:
                        after_exponential(pair, s + STEPS, 2)
                    if experts:
                        after_exponential(pair, s, 1)
                    if s == 1 and experts:
                        copy_sums(pair, -1)
                    if s == HSTEPS + 1 and attention:
                        copy_sums(pair, 0)

            over_pairs(act, body)

        @block.vector
        def _(dve):
            def max_step(pair, s):
                head, c, j = s // HSTEPS, s % HSTEPS // QC, s % QC
                par = head % 2
                wait(dve, max_ps, pair(STEPS, s + 1))
                if s % HSTEPS == 0:
                    wait(dve, fold_done, pair(2, head - 1))
                nc.vector.tensor_reduce(blockmax[:, par, c, j:j + 1], ps_m[s % 2][:], AX.X,
                                        ALU.max).then_inc(max_done, 1)

            def row_maxima(pair, head, step):
                par = head % 2
                if step == 0:
                    wait(dve, max_done, pair(STEPS, HSTEPS * (head + 1)))
                    wait(dve, fold_t, pair(2, head))
                    nc.vector.tensor_reduce(rowmax[:, 0:KEYB], blockmax[:, par], AX.X, ALU.max).then_inc(fold_done, 1)
                    wait(dve, fold_done, pair(2, head + 1))
                    wait(dve, negr_done, pair(2, head))
                    nc.vector.transpose(rowmax_t[:], rowmax[:]).then_inc(fold_t, 1)
                if step == 1:
                    wait(dve, fold_t, pair(2, head + 1))
                    wait(dve, m_ready, pair(2, head))
                    nc.vector.tensor_scalar(negmax[:], rowmax_t[:], -1.0, None, ALU.mult).then_inc(neg_done, 1)
                    wait(dve, neg_done, pair(2, head + 1))
                    wait(dve, mrow_landed[par], pair(MROW_SEM, MROW_SEM * (head // 2)))
                    nc.vector.tensor_copy(m_parts[:, par, 0, :], negmax[:]).then_inc(m1_done, 1)
                if step == 2:
                    wait(dve, m1_done, pair(2, head + 1))
                    nc.vector.tensor_tensor(negmax_r[:], negmax[:], m_parts[:, par, 0, :],
                                            ALU.subtract).then_inc(negr_done, 1)
                    wait(dve, negr_done, pair(2, head + 1))
                    nc.vector.tensor_copy(m_parts[:, par, 1, :], negmax_r[:]).then_inc(m2_done, 1)
                if step == 3:
                    wait(dve, m2_done, pair(2, head + 1))
                    nc.vector.tensor_tensor(m_parts[:, par, 2, :], negmax_r[:], m_parts[:, par, 1, :],
                                            ALU.subtract).then_inc(m_ready, 1)

            def per_tile(v):
                return v[:].unsqueeze(2).to_broadcast([P, 4, EXPERTS])

            def expert_steps(f, t, back):
                def at(each, more):
                    return f(each, more - back * each)

                def after(name, each=1, more=1):
                    wait(dve, S[name], at(each, more))

                vec = nc.vector
                tt, ts = nc.vector.tensor_tensor, nc.vector.tensor_scalar
                if t == 13:
                    after("xres_done")
                    for c in range(4):
                        last = vec.bn_stats(stats[:, c, :], x_res[:, c, :])
                    last.then_inc(S["st_done"], 1)
                if t == 15:
                    for c in range(4):
                        last = vec.bn_aggr(mv[:, c, :], stats[:, c, :])
                    last.then_inc(S["mv_done"], 1)
                if t == 16:
                    after("mv_done")
                    ts(ve[:], mv[:, :, 1], EPS, None, ALU.add).then_inc(S["ve_done"], 1)
                if t == 18:
                    after("rs_done")
                    for c in range(4):
                        last = ts(x_hat[:, c, :], x_res[:, c, :], mv[:, c, 0:1], rstd[:, c:c + 1],
                                  ALU.subtract, ALU.mult)
                    last.then_inc(S["xhat_done"], 1)
                if t == 22:
                    after("xth_done")
                    after("l_moved", 1, 0)
                    tt(next_l[:], ps_u[:], next_h[:].bitcast(F32), ALU.subtract).then_inc(S["xtl_done"], 1)
                if t == 26:
                    after("logit_done")
                    vec.tensor_reduce(top1[:], logits[:], AX.X, ALU.max).then_inc(S["top1_done"], 1)
                if t == 27:
                    after("top1_done")
                    tt(hit1[:], logits[:], per_tile(top1), ALU.is_equal).then_inc(S["hit1_done"], 1)
                    after("hit1_done")
                    tt(sel1[:], hit1[:], rank[:], ALU.mult).then_inc(S["pick1_done"], 1)
                if t == 28:
                    after("pick1_done")
                    vec.tensor_reduce(rank1[:], sel1[:], AX.X, ALU.max).then_inc(S["rank1_done"], 1)
                    after("rank1_done")
                    tt(hit1[:], sel1[:], per_tile(rank1), ALU.is_equal).then_inc(S["sel1_done"], 1)
                if t == 29:
                    after("sel1_done")
                    vec.scalar_tensor_tensor(out=rest[:], in0=hit1[:], scalar=-3.0e38, in1=logits[:],
                                             op0=ALU.mult, op1=ALU.add).then_inc(S["rest_done"], 1)
                    after("rest_done")
                    vec.tensor_reduce(top2[:], rest[:], AX.X, ALU.max).then_inc(S["top2_done"], 1)
                if t == 30:
                    after("top2_done")
                    tt(gap[:], top2[:], top1[:], ALU.subtract).then_inc(S["gap_done"], 1)
                    tt(hit2[:], rest[:], per_tile(top2), ALU.is_equal).then_inc(S["hit2_done"], 1)
                    after("hit2_done")
                    tt(sel2[:], hit2[:], rank[:], ALU.mult).then_inc(S["pick2_done"], 1)
                if t == 31:
                    after("pick2_done")
                    vec.tensor_reduce(rank2[:], sel2[:], AX.X, ALU.max).then_inc(S["rank2_done"], 1)
                    after("rank2_done")
                    tt(hit2[:], sel2[:], per_tile(rank2), ALU.is_equal).then_inc(S["sel2_done"], 1)
                if t == 32:
                    after("gexp_done")
                    ts(gate_sum[:], gap_exp[:], 1.0, None, ALU.add).then_inc(S["gsum_done"], 1)
                    after("gsum_done")
                    vec.reciprocal(gate1[:], gate_sum[:]).then_inc(S["gate1_done"], 1)
                if t == 33:
                    after("gate1_done")
                    tt(gate2[:], gate1[:], gap_exp[:], ALU.mult).then_inc(S["gate2_done"], 1)
                    tt(sel1[:], hit1[:], per_tile(gate1), ALU.mult).then_inc(S["mix1_done"], 1)
                if t == 34:
                    after("gate2_done")
                    after("sel2_done")
                    tt(sel2[:], hit2[:], per_tile(gate2), ALU.mult).then_inc(S["mix2_done"], 1)
                    after("mix1_done")
                    after("mix2_done")
                    tt(comb[:], sel1[:], sel2[:], ALU.add).then_inc(S["comb_done"], 1)
                if t == 38:
                    after("comb_t_done")
                    after("bcast_ps", EXPERTS, 0)
                    vec.tensor_copy(comb3[0:EXPERTS, :], comb_t).then_inc(S["comb1_done"], 1)
                if t == 39:
                    after("comb1_done")
                    tt(comb_r[:], comb_t, comb3[0:EXPERTS, :], ALU.subtract).then_inc(S["comb_r_done"], 1)
                if t == FIRST:
                    after("up_ps", FT, 0)
                    after("xth_done")
                    vec.tensor_copy(xt_h[:], next_h[:]).then_inc(S["h_moved"], 1)
                if t == 42:
                    after("comb_r_done")
                    vec.tensor_copy(comb_m[:], comb_r[:]).then_inc(S["comb2_done"], 1)
                if t == 43:
                    after("comb2_done")
                    vec.tensor_copy(comb3[32:32 + EXPERTS, :], comb_m[:]).then_inc(S["comb3_done"], 1)
                    tt(comb3[64:64 + EXPERTS, :], comb_r[:], comb_m[:], ALU.subtract).then_inc(S["comb3_done"], 1)
                e = (t - FIRST - 23) // 16
                if 0 <= e < EXPERTS and (t - FIRST - 23) % 16 == 0:
                    after("y_ps", FT, HC * (e + 1))
                    after("bcast_done", EXPERTS, e + 1)
                    after("y_done", EXPERTS, e)
                    tt(y_scaled, ps_y[:], comb_b[:, e % 2, :], ALU.mult).then_inc(S["y_scaled_done"], 1)

            def before_max(f, t, back):
                def at(each, more):
                    return f(each, more - back * each)

                def after(name, each=1, more=1):
                    wait(dve, S[name], at(each, more))

                vec = nc.vector
                tt, ts = nc.vector.tensor_tensor, nc.vector.tensor_scalar
                n, kind = (t - FIRST) // PER_TILE - 1, (t - FIRST) % PER_TILE
                if 0 <= n < FT and kind == 0:
                    after("gate_done", FT, n + 1)
                    vec.scalar_tensor_tensor(out=hid[:, n % 2, :], in0=hid[:, n % 2, :], scalar=1.0,
                                             in1=gate[:, n % 2, :], op0=ALU.add, op1=ALU.mult
                                             ).then_inc(S["silu_done"], 1)
                if 0 <= n < FT and kind == 1:
                    after("up_ps", FT, n + 1)
                    after("silu_done", FT, n + 1)
                    vec.scalar_tensor_tensor(out=hid[:, n % 2, :], in0=ps_u[:], scalar=b0_c[:, n:n + 1],
                                             in1=hid[:, n % 2, :], op0=ALU.add, op1=ALU.mult
                                             ).then_inc(S["hid_done"], 1)
                if t in (6, 10):
                    half = (t - 6) // 4
                    after("o_turned", 2, half + 1)
                    sums = ps_u[:].rearrange("p (a c j) -> p a c j", a=4, j=VW)
                    vec.reciprocal(inv_den[:, 4 * half:4 * half + 4, :], sums[:, :, :, DK]).then_inc(S["den_done"], 1)
                    after("den_done", 2, half + 1)
                    dst = x_hat[:].rearrange("p c (a j) -> p a c j", j=DK)
                    for a in range(4):
                        inv = inv_den[:, 4 * half + a, :].unsqueeze(2).to_broadcast([P, 4, DK])
                        last = tt(dst[:, 4 * half + a], sums[:, a, :, 0:DK], inv, ALU.mult)
                    last.then_inc(S["att_done"], 1)
                if t == 26:
                    after("logit_ps")
                    tt(logits[:], ps_u[:, 0:4 * EXPERTS].rearrange("p (c e) -> p c e", c=4),
                       bg_b[:].unsqueeze(1).to_broadcast([P, 4, EXPERTS]), ALU.add).then_inc(S["logit_done"], 1)
                if t == 38:
                    after("comb_ps")
                    vec.tensor_copy(comb_t, ps_u[0:EXPERTS, :]).then_inc(S["comb_t_done"], 1)
                if t == FIRST + 14 + STEPS:
                    after("final_ps")
                    after("base_done")
                    tt(out_sb[:], ps_u[:].rearrange("p (c d) -> p c d", c=4), out_sb[:],
                       ALU.add).then_inc(S["out_done"], 1)

            def body(pair, attention, experts, tail):
                for s in range(STEPS):
                    if tail:
                        before_max(pair, s + STEPS, 2)
                    if experts:
                        before_max(pair, s, 1)
                    if experts and s == 15:
                        wait(dve, S["st_done"], pair(1, 0))
                    if attention and has_max(pair, s):
                        m = s + AHEAD
                        max_step(pair, m)
                        for step in range(4):
                            if m % HSTEPS == (HSTEPS - 1 + step) % HSTEPS:
                                row_maxima(pair, (m - step) // HSTEPS, step)
                    if tail:
                        expert_steps(pair, s + STEPS, 2)
                    if experts:
                        expert_steps(pair, s, 1)
                    if attention and not has_max(pair, s) and has_max(pair, s - 3):
                        for step in range(1, 4):
                            if (s + AHEAD - step) % HSTEPS == HSTEPS - 1:
                                row_maxima(pair, (s + AHEAD - step) // HSTEPS, step)

            nc.vector.memset(k_exp[ROWS:ROWS + 3, :, :], 1.0).then_inc(ones_done, 1)
            nc.vector.memset(rowmax[:, KEYB:], 0.0).then_inc(ones_done, 1)
            dve.wait_ge(ones_done, 2)
            start = Pair(dve, 0)
            for s in range(AHEAD):
                max_step(start, s)
                for step in range(4):
                    if s == HSTEPS - 1 + step:
                        row_maxima(start, 0, step)
            over_pairs(dve, body)

        @block.gpsimd
        def _(pool):
            def expert_steps(f, t, back):
                def at(each, more):
                    return f(each, more - back * each)

                if t == 11:
                    wait(pool, S["att_done"], at(2, 2))
                    wait(pool, S["base_done"], at(1, 0))
                    wait(pool, S["xin_landed"], at(32, 32))
                    nc.gpsimd.tensor_tensor(x_res[:], x_hat[:], x_in[:], ALU.add).then_inc(S["xres_done"], 1)
                if t == 16:
                    wait(pool, S["ve_done"], at(1, 1))
                    nc.gpsimd.tensor_tensor(rstd[:], ve[:], exponent[:, 0:4], ALU.pow).then_inc(S["rs_done"], 1)
                n = (t - FIRST) // PER_TILE - 1
                if 0 <= n < FT and (t - FIRST) % PER_TILE == 1:
                    wait(pool, S["hi_done"], at(FT, n + 1))
                    nc.gpsimd.tensor_tensor(hid_l[:, n % 2, :], hid[:, n % 2, :], hid_h[:, n % 2, :].bitcast(F32),
                                            ALU.subtract).then_inc(S["lo_done"], 1)
                e = (t - FIRST - 23) // 16
                if 0 <= e < EXPERTS and (t - FIRST - 23) % 16 == 0:
                    wait(pool, S["y_scaled_done"], at(EXPERTS, e + 1))
                    wait(pool, S["y_done"], at(EXPERTS, e))
                    if e == 0:
                        wait(pool, S["y_init"], at(1, 1))
                    nc.gpsimd.tensor_tensor(y_sum, y_sum, y_scaled, ALU.add).then_inc(S["y_done"], 1)

            def body(pair, attention, experts, tail):
                for s in range(STEPS):
                    if tail:
                        expert_steps(pair, s + STEPS, 2)
                    if experts:
                        expert_steps(pair, s, 1)

            def load(i):
                w, e = i // EXPERTS, i % EXPERTS
                if i >= 2:
                    pool.wait_ge(w_done, i - 1)
                src = (W0[e], W1[e], W2[e].rearrange("(c p) d -> p c d", p=P))[w]
                dst = w_raw[:, i % 2, :]
                if w == 2:
                    dst = dst.rearrange("p (c d) -> p c d", c=HC)
                pool.dma_start(dst, src).then_inc(w_landed[i % 2], 16)

            load(0)
            for i in range(3 * EXPERTS):
                if i + 1 < 3 * EXPERTS:
                    load(i + 1)
                w, e = i // EXPERTS, i % EXPERTS
                pool.wait_ge(w_landed[i % 2], 16 * (i // 2 + 1))
                nc.gpsimd.tensor_scalar(w_h[w][:, e, :], w_raw[:, i % 2, :], 1.0, 0.0, ALU.mult,
                                        ALU.add).then_inc(wh_done, 1)
                pool.wait_ge(wh_done, i + 1)
                nc.gpsimd.tensor_tensor(w_l[w][:, e, :], w_raw[:, i % 2, :], w_h[w][:, e, :].bitcast(F32),
                                        ALU.subtract).then_inc(w_done, 1)
            over_pairs(pool, body)


def block_kernel(nc, x, Wq, bq, Wk, bk, Wv, bv, gamma, beta, Wg, bg, W0, b0, W1, b1, W2, b2, out):
    parts_d = nc.dram_tensor("parts_scratch", [2, 3, BATCH, P, SEQ], BF16).ap()
    values_d = nc.dram_tensor("values_scratch", [BATCH, HEADS, P, KEYB * VW], F32).ap()
    with ExitStack() as ctx:
        def sb(name, shape, dt=F32):
            return ctx.enter_context(nc.sbuf_tensor(name, shape, dt))

        keep = (sb("ident", [P, P]), sb("rank", [P, 4, EXPERTS]), sb("bg_b", [P, EXPERTS]),
                sb("wg_h", [P, EXPERTS], F32R), sb("wg_l", [P, EXPERTS], F32R),
                sb("b0_c", [P, FT]), sb("b1_c", [P, FT]), sb("b1h_c", [P, FT]),
                sb("b2_sb", [EXPERTS, D]), sb("sel", [96, EXPERTS, P], BF16), sb("comb3", [96, 512], BF16),
                sb("exponent", [P, 4]))
        setup_stage(nc, (x, Wq, bq, Wk, bk, Wv, bv, gamma, beta, Wg, bg, b0, b1, b2), (parts_d, values_d), keep)
        main_stage(nc, x, (W0, W1, W2), out, (parts_d, values_d), keep)


_INS = ["L0_attn_x", "L0_attn_Wq", "L0_attn_bq", "L0_attn_Wk", "L0_attn_bk", "L0_attn_Wv", "L0_attn_bv",
        "L0_attn_gamma", "L0_attn_beta", "L0_ffn_Wg", "L0_ffn_bg", "L0_ffn_W0", "L0_ffn_b0", "L0_ffn_W1",
        "L0_ffn_b1", "L0_ffn_W2", "L0_ffn_b2"]


def kernel(**inputs):
    import numpy as _np
    import concourse.bacc as _bacc
    from concourse import mybir as _mybir
    from concourse.bass_utils import run_bass_kernel_spmd as _run

    nc = _bacc.Bacc("TRN2", target_bir_lowering=False, num_devices=1)
    arrays, args = {}, []
    for name in _INS:
        a = _np.ascontiguousarray(inputs[name])
        arrays[f"in_{name}_dram"] = a
        args.append(nc.dram_tensor(f"in_{name}_dram", a.shape, _mybir.dt.from_np(a.dtype), kind="ExternalInput").ap())
    out = nc.dram_tensor("out_dram", (BATCH, SEQ, D), F32, kind="ExternalOutput").ap()
    block_kernel(nc, *args, out)
    r = _run(nc, [arrays], core_ids=[0])
    return r.results[0]["out_dram"]
```

```python
from contextlib import ExitStack

import concourse.bass as bass
from concourse import mybir

ALU = mybir.AluOpType
ACT = mybir.ActivationFunctionType
AX = mybir.AxisListType
F32 = mybir.dt.float32
F32R = mybir.dt.float32r
BF16 = mybir.dt.bfloat16

P = 128
BATCH, SEQ, D = 2, 2048, 128
HEADS, DK = 8, 16
EXPERTS, HID = 8, 512
EPS = 1e-5
TOKENS = BATCH * SEQ
TILES = TOKENS // P
GROUPS = TILES // 4
NHEADS = BATCH * HEADS
PAIRS = NHEADS // 2
KEYB = SEQ // P
QC = SEQ // 512
STEPS = 2 * KEYB * QC
HSTEPS = STEPS // 2
VW = 32
PRODUCTS = ((0, 0), (0, 1), (0, 2), (1, 0), (1, 1), (2, 0))
ROWS = DK * len(PRODUCTS)
LEAD = 5
AHEAD = (KEYB + LEAD) * QC
EARLY = 14
HC = HID // P
FT = EXPERTS * HC
PER_TILE = STEPS // FT
FIRST = 40
TILES_BESIDE = (STEPS - FIRST) // PER_TILE
STACK_SEM = 16 * 2 * 3
MROW_SEM = 16 * 3 * 4


def wait(eng, sem, n):
    if isinstance(n, tuple):
        base, more, level = n
        if more:
            eng.reg_add(level, base, more)
        eng.wait_ge(sem, level if more else base)
    elif n > 0:
        eng.wait_ge(sem, n)


class Pair:

    def __init__(self, eng, p, bases=None):
        self.eng, self.p, self.bases = eng, p, bases

    def __call__(self, each, more):
        if isinstance(self.p, int):
            return self.p * each + more
        return self.bases[each], more, self.bases["level"]

    def number(self, each, more):
        return self.p * each + more


RATES = sorted({1, 2, 3, 4, 8, 16, 32, STEPS, STACK_SEM, MROW_SEM})


def over_pairs(eng, body):
    body(Pair(eng, 0), True, False, False)
    body(Pair(eng, 1), True, True, False)
    bases = {each: eng.alloc_register(f"pairs_times_{each}") for each in RATES}
    bases["level"] = eng.alloc_register("level")
    with eng.Fori(2, PAIRS - 1) as p:
        for each in RATES:
            eng.reg_mov(bases[each], p * each)
        body(Pair(eng, p, bases), True, True, True)
    body(Pair(eng, PAIRS - 1), True, True, True)
    body(Pair(eng, PAIRS), False, True, True)
    body(Pair(eng, PAIRS + 1), False, False, True)


def has_max(pair, s):
    return not isinstance(pair.p, int) or 2 * pair.p + (s + AHEAD) // HSTEPS < NHEADS


def in_groups(step, g):
    if 0 <= g < GROUPS:
        step(g)


def load_stack(sp, parts_d, q, k, par, head, landed):
    for part, row, times in ((0, 0, 3), (1, 3 * DK, 2), (2, 5 * DK, 1)):
        end = row + DK * times
        sp.dma_start(q[row:end, par, :], parts_d[0, head, part:part + 1].to_broadcast([times, DK, SEQ])
                     ).then_inc(landed[par], 16)
        sp.dma_start(k[row:end, par, :], parts_d[1, head, 0:times]).then_inc(landed[par], 16)


def load_values(sp, values_d, values, par, head, landed):
    sp.dma_start(values[:, par].rearrange("p k v -> p (k v)"),
                 values_d.rearrange("b h p v -> (b h) p v")[head]).then_inc(landed[par], 16)


def setup_stage(nc, io, scratch, keep, stacks):
    (x, Wq, bq, Wk, bk, Wv, bv, gamma, beta, Wg, bg, b0, b1, b2) = io
    parts_d, values_d = scratch
    (ident, rank, bg_b, wg_hl, b0_c, b1_c, b1h_c, b2_sb, sel, comb3, exponent) = keep
    (q_max, k_max, q_exp, k_exp, values, blockmax, max_ps, max_done, max_landed, exp_landed, values_landed) = stacks
    with ExitStack() as ctx:
        def sb(name, shape, dt=F32):
            return ctx.enter_context(nc.sbuf_tensor(name, shape, dt))

        def sem(name):
            return ctx.enter_context(nc.semaphore(name))

        xs = sb("xs", [P, TILES, D])
        xt = sb("xt", [P, TOKENS])
        wq, wk = sb("wq", [P, D]), sb("wk", [P, D])
        wv = sb("wv", [P, HEADS * D])
        wv_sum = sb("wv_sum", [P, D])
        bv_b = sb("bv_b", [P, HEADS * D])
        bv_sum = sb("bv_sum", [P, D])
        gamma_c, beta_c = sb("gamma_c", [P, 1]), sb("beta_c", [P, 1])
        bq_c, bk_c = sb("bq_c", [P, 1]), sb("bk_c", [P, 1])
        wg = sb("wg", [P, EXPERTS])
        b_rows = sb("b_rows", [FT, 2, P])
        stats = sb("stats", [P, TILES, 6])
        mv = sb("mv", [P, TILES, 2])
        ve = sb("ve", [P, TILES])
        rstd = sb("rstd", [P, TILES])
        part = [[sb(f"part{w}{i}", [P, BATCH, SEQ], BF16) for i in range(3)] for w in "qk"]
        qf, kf = sb("qf", [P, 2, 512]), sb("kf", [P, 2, 512])
        qr, kr = sb("qr", [P, 2, 512]), sb("kr", [P, 2, 512])
        vh = sb("vh", [P, BATCH, HEADS, KEYB, VW])
        ps_t, ps_q, ps_k, ps_v = [
            [ctx.enter_context(nc.psum_tensor(f"ps_{n}{i}", [P, 512], F32)) for i in range(2)]
            for n in "tqkv"]

        x_landed = [sem(f"x_landed{g}") for g in range(GROUPS)]
        qkw_landed, wv_landed, cols_landed = sem("qkw_landed"), sem("wv_landed"), sem("cols_landed")
        keep_landed = sem("keep_landed")
        sums_done, stats_done, mv_done, ve_done = sem("sums_done"), sem("stats_done"), sem("mv_done"), sem("ve_done")
        rstd_done, xhat_done, tr_done, xt_done = sem("rstd_done"), sem("xhat_done"), sem("tr_done"), sem("xt_done")
        q_ps, k_ps, v_ps = sem("q_ps"), sem("k_ps"), sem("v_ps")
        qf_done, q1_done, qr_done, q2_done, q3_done = [sem(f"{n}_done") for n in ("qf", "q1", "qr", "q2", "q3")]
        kf_done, k1_done, kr_done, k2_done, k3_done = [sem(f"{n}_done") for n in ("kf", "k1", "kr", "k2", "k3")]
        v_done, vh_zero, vh_one, ident_zero, ident_done, const_zero, const_done = [
            sem(n) for n in ("v_done", "vh_zero", "vh_one", "ident_zero", "ident_done", "const_zero", "const_done")]
        wgh_done, wgl_done, b_cols, b1h_done = [
            sem(n) for n in ("wgh_done", "wgl_done", "b_cols", "b1h_done")]
        parts_written, values_written = [[sem(f"{n}_written{b}") for b in range(BATCH)] for n in ("parts", "values")]

        x_t = x.rearrange("b (n p) d -> p (b n) d", p=P)

        def col(v):
            return v.rearrange("(p a) -> p a", a=1)

        with nc.Block() as block:
            @block.sync
            def _(sp):
                for g in range(GROUPS):
                    sp.dma_start(xs[:, 4 * g:4 * g + 4, :], x_t[:, 4 * g:4 * g + 4, :]).then_inc(x_landed[g], 16)
                for b in range(BATCH):
                    heads = slice(HEADS * b, HEADS * b + HEADS)
                    for first, groups in ((0, 2), (2, 1), (3, 1)):
                        done = 4 * b + first + groups
                        cols = slice(512 * first, 512 * (first + groups))
                        for i, (sq, sk) in enumerate(((q1_done, k1_done), (q2_done, k2_done), (q3_done, k3_done))):
                            for w, part_done in ((0, sq), (1, sk)):
                                sp.wait_ge(part_done, done)
                                sp.dma_start(parts_d[w, heads, i, :, cols], part[w][i][:, b, cols]
                                             ).then_inc(parts_written[b], 16)
                        if b == 0 and first == 3:
                            sp.wait_ge(parts_written[0], 16 * 6 * 3)
                            load_stack(sp, parts_d, q_max, k_max, 0, 0, max_landed)
                        sp.wait_ge(v_done, done)
                        keys = slice(4 * first, 4 * (first + groups))
                        sp.dma_start(values_d[b].rearrange("h p (k v) -> p h k v", v=VW)[:, :, keys, :],
                                     vh[:, b, :, keys, :]).then_inc(values_written[b], 16)
                sp.wait_ge(values_written[0], 16 * 3)
                sp.wait_ge(parts_written[1], 16 * 6 * 3)
                sp.wait_ge(values_written[1], 16 * 3)
                sp.wait_ge(keep_landed, 16 * 4)

            @block.gpsimd
            def _(pool):
                nc.gpsimd.memset(ident[:], 0.0).then_inc(ident_zero, 1)
                pool.wait_ge(ident_zero, 1)
                nc.gpsimd.affine_select(out=ident[:], in_=ident[:], compare_op=ALU.not_equal, fill=1.0, base=0,
                                        pattern=[[-1, P]], channel_multiplier=1).then_inc(ident_done, 1)
                nc.gpsimd.memset(exponent[:], -0.5).then_inc(const_done, 1)
                nc.gpsimd.memset(vh[:, :, :, :, DK + 1:VW], 0.0).then_inc(vh_one, 1)
                nc.gpsimd.memset(vh[:, :, :, :, DK:DK + 1], 1.0).then_inc(vh_one, 1)
                pool.wait_ge(const_done, 1)

                def rsqrt(g):
                    pool.wait_ge(ve_done, g + 1)
                    nc.gpsimd.tensor_tensor(rstd[:, 4 * g:4 * g + 4], ve[:, 4 * g:4 * g + 4],
                                            exponent[:, 0:4], ALU.pow).then_inc(rstd_done, 1)

                def key_rest(g):
                    b, c = g // 4, 512 * (g % 4)
                    pool.wait_ge(k1_done, g + 1)
                    nc.gpsimd.tensor_tensor(kr[:, g % 2, :], kf[:, g % 2, :], part[1][0][:, b, c:c + 512],
                                            ALU.subtract).then_inc(kr_done, 1)

                def key_part3(g):
                    b, c = g // 4, 512 * (g % 4)
                    pool.wait_ge(k2_done, g + 1)
                    nc.gpsimd.tensor_tensor(part[1][2][:, b, c:c + 512], kr[:, g % 2, :],
                                            part[1][1][:, b, c:c + 512], ALU.subtract).then_inc(k3_done, 1)

                def constants():
                    nc.gpsimd.memset(sel[:], 0.0).then_inc(const_zero, 1)
                    nc.gpsimd.memset(comb3[:], 0.0)
                    for e in range(EXPERTS):
                        nc.gpsimd.memset(rank[:, :, e:e + 1], float(EXPERTS - e))
                    for part_no in range(3):
                        pool.wait_ge(const_zero, part_no + 1)
                        nc.gpsimd.affine_select(out=sel[:], in_=sel[:], compare_op=ALU.not_equal, fill=1.0,
                                                base=-32 * part_no, pattern=[[-1, EXPERTS], [0, P]],
                                                channel_multiplier=1).then_inc(const_zero, 1)
                    pool.wait_ge(const_zero, 4)

                for i in range(-3, GROUPS + 1):
                    if i == 0:
                        constants()
                    in_groups(key_rest, i - 1)
                    in_groups(rsqrt, i + 3)
                    in_groups(key_part3, i - 1)

            @block.scalar
            def _(act):
                act.dma_start(wq[:], Wq).then_inc(qkw_landed, 16)
                act.dma_start(wk[:], Wk).then_inc(qkw_landed, 16)
                for dst, src in ((gamma_c, gamma), (beta_c, beta), (bq_c, bq), (bk_c, bk)):
                    act.dma_start(dst[:], col(src)).then_inc(cols_landed, 16)
                act.dma_start(wg[:], Wg).then_inc(cols_landed, 16)
                act.dma_start(wv[:], Wv).then_inc(wv_landed, 16)
                act.dma_start(bv_b[:], bv.partition_broadcast(P)).then_inc(wv_landed, 16)
                act.dma_start(bg_b[:], bg.partition_broadcast(P)).then_inc(keep_landed, 16)
                act.dma_start(b_rows[:, 0, :], b0.rearrange("e (c p) -> (e c) p", p=P)).then_inc(keep_landed, 16)
                act.dma_start(b_rows[:, 1, :], b1.rearrange("e (c p) -> (e c) p", p=P)).then_inc(keep_landed, 16)
                act.dma_start(b2_sb[:], b2).then_inc(keep_landed, 16)
                act.wait_ge(cols_landed, 16 * 5)

                def norm_out(g):
                    act.wait_ge(tr_done, g + 1)
                    nc.scalar.activation(xt[:, 512 * g:512 * g + 512], ps_t[g % 2][:], ACT.Identity,
                                         bias=beta_c[:], scale=gamma_c[:]).then_inc(xt_done, 1)

                def key_out(g):
                    act.wait_ge(k_ps, g + 1)
                    if g >= 2:
                        act.wait_ge(kr_done, g - 1)
                    nc.scalar.activation(kf[:, g % 2, :], ps_k[g % 2][:], ACT.Identity,
                                         bias=bk_c[:]).then_inc(kf_done, 1)

                def first_parts(g):
                    b, c = g // 4, 512 * (g % 4)
                    act.wait_ge(qf_done, g + 1)
                    nc.scalar.activation(part[0][0][:, b, c:c + 512], qf[:, g % 2, :], ACT.Copy).then_inc(q1_done, 1)
                    act.wait_ge(kf_done, g + 1)
                    nc.scalar.activation(part[1][0][:, b, c:c + 512], kf[:, g % 2, :], ACT.Copy).then_inc(k1_done, 1)

                def second_parts(g):
                    b, c = g // 4, 512 * (g % 4)
                    act.wait_ge(qr_done, g + 1)
                    nc.scalar.activation(part[0][1][:, b, c:c + 512], qr[:, g % 2, :], ACT.Copy).then_inc(q2_done, 1)
                    act.wait_ge(kr_done, g + 1)
                    nc.scalar.activation(part[1][1][:, b, c:c + 512], kr[:, g % 2, :], ACT.Copy).then_inc(k2_done, 1)

                for i in range(-3, GROUPS + 1):
                    in_groups(key_out, i - 1)
                    in_groups(first_parts, i - 1)
                    in_groups(norm_out, i + 1)
                    in_groups(second_parts, i - 1)
                act.wait_ge(b_cols, 1)
                nc.scalar.activation(b0_c[:], ps_t[0][:, 0:FT], ACT.Copy)
                nc.scalar.activation(b1_c[:], ps_t[0][:, FT:2 * FT], ACT.Copy)
                nc.scalar.mul(b1h_c[:], ps_t[0][:, FT:2 * FT], 0.5).then_inc(b1h_done, 1)

            @block.vector
            def _(dve):
                nc.vector.memset(k_exp[ROWS:ROWS + 3, :, :], 1.0)

                def statistics(g):
                    dve.wait_ge(x_landed[g], 16)
                    for j in range(4 * g, 4 * g + 4):
                        last = nc.vector.bn_stats(stats[:, j, :], xs[:, j, :])
                    last.then_inc(stats_done, 1)

                def moments(g):
                    dve.wait_ge(stats_done, g + 1)
                    for j in range(4 * g, 4 * g + 4):
                        last = nc.vector.bn_aggr(mv[:, j, :], stats[:, j, :])
                    last.then_inc(mv_done, 1)

                def variances(g):
                    dve.wait_ge(mv_done, g + 1)
                    nc.vector.tensor_scalar(ve[:, 4 * g:4 * g + 4], mv[:, 4 * g:4 * g + 4, 1], 1.0 + EPS, EPS * EPS,
                                            ALU.mult, ALU.add).then_inc(ve_done, 1)

                def normalise(g):
                    dve.wait_ge(rstd_done, g + 1)
                    for j in range(4 * g, 4 * g + 4):
                        last = nc.vector.tensor_scalar(xs[:, j, :], xs[:, j, :], mv[:, j, 0:1], rstd[:, j:j + 1],
                                                       ALU.subtract, ALU.mult)
                    last.then_inc(xhat_done, 1)

                def query_out(g):
                    dve.wait_ge(q_ps, g + 1)
                    if g >= 2:
                        dve.wait_ge(q1_done, g - 1)
                        dve.wait_ge(qr_done, g - 1)
                    nc.vector.tensor_scalar(qf[:, g % 2, :], ps_q[g % 2][:], bq_c[:], float(DK) ** -0.5,
                                            ALU.add, ALU.mult).then_inc(qf_done, 1)

                def values_out(g):
                    dve.wait_ge(v_ps, g + 1)
                    k = 4 * (g % 4)
                    bias = bv_sum[:].rearrange("p (h v) -> p h v", v=DK).unsqueeze(1)
                    nc.vector.tensor_tensor(vh[:, g // 4, :, k:k + 4, 0:DK].rearrange("p h k v -> p k h v"),
                                            ps_v[g % 2][:].rearrange("p (k h v) -> p k h v", k=4, v=DK),
                                            bias.to_broadcast([P, 4, HEADS, DK]), ALU.add).then_inc(v_done, 1)

                def query_rest(g):
                    b, c = g // 4, 512 * (g % 4)
                    dve.wait_ge(q1_done, g + 1)
                    if g >= 2:
                        dve.wait_ge(q2_done, g - 1)
                        dve.wait_ge(q3_done, g - 1)
                    nc.vector.tensor_tensor(qr[:, g % 2, :], qf[:, g % 2, :], part[0][0][:, b, c:c + 512],
                                            ALU.subtract).then_inc(qr_done, 1)

                def query_part3(g):
                    b, c = g // 4, 512 * (g % 4)
                    dve.wait_ge(q2_done, g + 1)
                    dve.wait_ge(qr_done, g + 1)
                    nc.vector.tensor_tensor(part[0][2][:, b, c:c + 512], qr[:, g % 2, :],
                                            part[0][1][:, b, c:c + 512], ALU.subtract).then_inc(q3_done, 1)

                for i in range(-3, GROUPS + 1):
                    in_groups(query_out, i - 1)
                    in_groups(statistics, i + 3)
                    in_groups(query_rest, i - 1)
                    in_groups(moments, i + 3)
                    if i - 1 == 0:
                        dve.wait_ge(sums_done, 2)
                        dve.wait_ge(vh_one, 2)
                    in_groups(values_out, i - 1)
                    in_groups(variances, i + 3)
                    in_groups(normalise, i + 2)
                    in_groups(query_part3, i - 1)
                    if i == -3:
                        dve.wait_ge(wv_landed, 32)
                        nc.vector.tensor_reduce(wv_sum[:], wv[:].rearrange("p (j n) -> p j n", n=HEADS), AX.X,
                                                ALU.add).then_inc(sums_done, 1)
                        nc.vector.tensor_reduce(bv_sum[:], bv_b[:].rearrange("p (j n) -> p j n", n=HEADS), AX.X,
                                                ALU.add).then_inc(sums_done, 1)
                    if i == -1:
                        dve.wait_ge(cols_landed, 16 * 5)
                        nc.vector.tensor_copy(wg_hl[:, 0, :], wg[:]).then_inc(wgh_done, 1)
                dve.wait_ge(wgh_done, 1)
                nc.vector.tensor_tensor(wg_hl[:, 1, :], wg[:], wg_hl[:, 0, :].bitcast(F32), ALU.subtract).then_inc(wgl_done, 1)
                dve.wait_ge(wgl_done, 1)
                for s in range(EARLY):
                    dve.wait_ge(max_ps, s + 1)
                    nc.vector.tensor_reduce(blockmax[:, 0, s // QC, s % QC:s % QC + 1], (*ps_q, *ps_k)[s % 4][:],
                                            AX.X, ALU.max).then_inc(max_done, 1)

            @block.tensor
            def _(pe):
                def transposes(g):
                    pe.wait_ge(xhat_done, g + 1)
                    if g >= 2:
                        pe.wait_ge(xt_done, g - 1)
                    for j in range(4):
                        last = nc.tensor.transpose(ps_t[g % 2][:, P * j:P * j + P], xs[:, 4 * g + j, :], ident[:])
                    last.then_inc(tr_done, 1)

                pe.wait_ge(ident_done, 1)
                def projections(g):
                    if g == 0:
                        pe.wait_ge(qkw_landed, 32)
                        pe.wait_ge(sums_done, 1)
                    pe.wait_ge(xt_done, g + 1)
                    if g >= 2:
                        pe.wait_ge(qf_done, g - 1)
                    nc.tensor.matmul(ps_q[g % 2][:], wq[:], xt[:, 512 * g:512 * g + 512], start=True,
                                     stop=True).then_inc(q_ps, 1)
                    if g >= 2:
                        pe.wait_ge(kf_done, g - 1)
                    nc.tensor.matmul(ps_k[g % 2][:], wk[:], xt[:, 512 * g:512 * g + 512], start=True,
                                     stop=True).then_inc(k_ps, 1)
                    if g >= 2:
                        pe.wait_ge(v_done, g - 1)
                    for j in range(4):
                        last = nc.tensor.matmul(ps_v[g % 2][:, P * j:P * j + P],
                                                xt[:, 512 * g + P * j:512 * g + P * j + P], wv_sum[:],
                                                start=True, stop=True)
                    last.then_inc(v_ps, 1)

                for i in range(-3, GROUPS + 1):
                    in_groups(transposes, i + 1)
                    in_groups(projections, i)
                pe.wait_ge(keep_landed, 16 * 4)
                for i in range(2):
                    last = nc.tensor.transpose(ps_t[0][:, FT * i:FT * i + FT], b_rows[:, i, :], ident[0:FT, 0:FT])
                last.then_inc(b_cols, 1)
                pe.wait_ge(max_landed[0], STACK_SEM)
                pe.wait_ge(qf_done, GROUPS)
                pe.wait_ge(kf_done, GROUPS)
                for s in range(EARLY):
                    c, j = P * (s // QC), 512 * (s % QC)
                    if s >= 4:
                        pe.wait_ge(max_done, s - 3)
                    nc.tensor.matmul((*ps_q, *ps_k)[s % 4][:], q_max[0:ROWS, 0, c:c + P], k_max[0:ROWS, 0, j:j + 512],
                                     start=True, stop=True).then_inc(max_ps, 1)


def main_stage(nc, x, weights, out, scratch, keep, stacks):
    parts_d, values_d = scratch
    (ident, rank, bg_b, wg_hl, b0_c, b1_c, b1h_c, b2_sb, sel, comb3, exponent) = keep
    (q_max, k_max, q_exp, k_exp, values, blockmax, max_ps, max_done, max_landed, exp_landed, values_landed) = stacks
    W0, W1, W2 = weights
    with ExitStack() as ctx:
        def sb(name, shape, dt=F32):
            return ctx.enter_context(nc.sbuf_tensor(name, shape, dt))

        def sem(name):
            return ctx.enter_context(nc.semaphore(name))

        w_h = [sb(f"w{i}_h", [P, EXPERTS, 512], F32R) for i in range(3)]
        w_l = [sb(f"w{i}_l", [P, EXPERTS, 512], F32R) for i in range(3)]
        w_raw = sb("w_raw", [P, 2, 512])
        rowmax = sb("rowmax", [P, 32])
        rowmax_t = sb("rowmax_t", [P, 32])
        negmax = sb("negmax", [P, 32])
        negmax_r = sb("negmax_r", [P, 32])
        m_parts = sb("m_parts", [P, 2, 3, 32], BF16)
        probs = sb("probs", [P, 2, QC, 512])
        o_sb = sb("o_sb", [P, 2, 512])
        x_in = sb("x_in", [P, 4, D])
        x_res = sb("x_res", [P, 4, D])
        x_hat = sb("x_hat", [P, 4, D])
        inv_den = sb("inv_den", [P, 8, 4])
        stats = sb("stats2", [P, 4, 6])
        mv = sb("mv2", [P, 4, 2])
        ve = sb("ve2", [P, 4])
        rstd = sb("rstd2", [P, 4])
        next_h, next_l = sb("next_h", [P, 512], F32R), sb("next_l", [P, 512], F32R)
        xt_h, xt_l = sb("xt_h", [P, 512], F32R), sb("xt_l", [P, 512], F32R)
        logits = sb("logits", [P, 4, EXPERTS])
        top1, top2, rank1, rank2 = [sb(n, [P, 4]) for n in ("top1", "top2", "rank1", "rank2")]
        hit1, hit2, sel1, sel2, rest = [sb(n, [P, 4, EXPERTS]) for n in ("hit1", "hit2", "sel1", "sel2", "rest")]
        gap, gap_exp, gate_sum, gate1, gate2 = [sb(n, [P, 4]) for n in ("gap", "gap_exp", "gate_sum", "gate1", "gate2")]
        comb = sb("comb", [P, 4, EXPERTS])
        comb_t = x_in[0:EXPERTS].rearrange("p c d -> p (c d)")
        comb_m, comb_r = sb("comb_m", [EXPERTS, 512], BF16), sb("comb_r", [EXPERTS, 512])
        comb_b = sb("comb_b", [P, 2, 512])
        hid, gate = sb("hid", [P, 4, 512]), sb("gate", [P, 2, 512])
        hid_h, hid_l = sb("hid_h", [P, 2, 512], F32R), sb("hid_l", [P, 2, 512], F32R)
        y_sum, y_scaled = w_raw[:, 0, :], w_raw[:, 1, :]
        out_sb = sb("out_sb", [P, 4, D])

        ps_s = [ctx.enter_context(nc.psum_tensor(f"ps_s{i}", [P, 512], F32)) for i in range(2)]
        ps_m = [ctx.enter_context(nc.psum_tensor(f"ps_m{i}", [P, 512], F32)) for i in range(2)]
        ps_o, ps_g, ps_u, ps_y = [ctx.enter_context(nc.psum_tensor(n, [P, 512], F32))
                                  for n in ("ps_o", "ps_g", "ps_u", "ps_y")]

        mrow_landed = [sem(f"mrow_landed{i}") for i in range(2)]
        zero_done = sem("zero_done")
        fold_done, fold_t, neg_done, m1_done, negr_done, m2_done, m_ready = [
            sem(n) for n in ("fold_done", "fold_t", "neg_done", "m1_done", "negr_done", "m2_done", "m_ready")]
        score_ps, probs_done, pv_done, o_done = sem("score_ps"), sem("probs_done"), sem("pv_done"), sem("o_done")
        w_landed = [sem(f"w_landed{i}") for i in range(2)]
        wh_done, w_done = sem("wh_done"), sem("w_done")
        names = ("xin_landed o_turned den_done att_done xres_done st_done mv_done ve_done rs_done xhat_done xt_ps h_moved l_moved "
                 "xth_done xtl_done logit_ps lsum_done logit_done top1_done hit1_done pick1_done rank1_done sel1_done "
                 "rest_done top2_done hit2_done pick2_done rank2_done sel2_done gap_done gexp_done gsum_done "
                 "gate1_done gate2_done mix1_done mix2_done comb_done comb_ps comb_t_done comb1_done comb_r_done "
                 "comb2_done comb3_done b2_ps y_init bcast_ps bcast_done gate_ps up_ps gate_done "
                 "silu_done hid_done hi_done lo_done y_ps y_copied y_scaled_done y_done final_ps base_done out_done").split()
        S = {n: sem("e_" + n) for n in names}
        out_stored = sem("out_stored")

        x_pairs = x.rearrange("b s d -> (b s) d").rearrange("(f h c q) d -> f h q c d", h=2, c=4, q=64)
        out_pairs = out.rearrange("b s d -> (b s) d").rearrange("(f h c q) d -> f h q c d", h=2, c=4, q=64)

        def alone(f, back, n=0):
            return isinstance(f.p, int) and (f.p - back, n) >= (PAIRS - 2, TILES_BESIDE)

        def expert_summed(f, t, back):
            e = (t - FIRST - 24) // 16
            late = 1 if alone(f, back, HC * (e + 1)) else 0
            return e if 0 <= e < EXPERTS and (t - FIRST - 24 - late) % 16 == 0 else None

        def down_tile(f, t, back):
            late = alone(f, back, (t - FIRST) // PER_TILE)
            m, rest = divmod(t - FIRST - 10 - 2 * late, PER_TILE)
            done = late and f.p - back == PAIRS - 2 and m < TILES_BESIDE - 2
            return m if 0 <= m < FT and rest == 0 and not done else None

        def gate_bank(f, back, n):
            return ps_m[0] if alone(f, back, n) and n % 2 else ps_g

        def up_bank(f, back, n):
            return ps_m[1] if alone(f, back, n) and n % 2 else ps_u

        def max_bank(f, s):
            return (*ps_m, ps_g, ps_u)[s % 4] if beside_nothing(f) else ps_m[s % 2]

        def score_banks(f):
            return (*ps_s, ps_y) if beside_nothing(f) else ps_s

        def beside_nothing(f):
            return isinstance(f.p, int) and f.p == 0

        def y_bank(f, back, e):
            return ps_s[1] if alone(f, back, HC * e) and e % 2 else ps_y

        def scalar_splits(f, back, n):
            return alone(f, back, n + 1) and f.p - back == PAIRS - 2

        def other_bank(f):
            return ps_s[0] if isinstance(f.p, int) and f.p >= PAIRS else ps_u

        other_readers = {PAIRS: {5: ("bcast_done", 54), 9: ("att_done", 15), 17: ("att_done", 16),
                                 21: ("bcast_done", 55), 25: ("xtl_done", 8), 33: ("lsum_done", 8),
                                 37: ("bcast_done", 56), 49: ("comb_t_done", 8), 53: ("bcast_done", 57),
                                 57: ("out_done", 7), 65: ("y_init", 8), 81: ("bcast_done", 58),
                                 97: ("bcast_done", 59), 113: ("bcast_done", 60)},
                         PAIRS + 1: {1: ("bcast_done", 61), 17: ("bcast_done", 62), 33: ("bcast_done", 63),
                                     53: ("bcast_done", 64)}}

        block = ctx.enter_context(nc.Block())

        @block.sync
        def _(sp):
            def load_for_max(pair, h):
                wait(sp, max_ps, pair(STEPS, HSTEPS * (h - 1)))
                load_stack(sp, parts_d, q_max, k_max, h % 2, pair.number(2, h), max_landed)

            def load_for_exp(pair, h):
                wait(sp, score_ps, pair(STEPS, HSTEPS * (h - 1)))
                load_stack(sp, parts_d, q_exp, k_exp, h % 2, pair.number(2, h), exp_landed)
                wait(sp, pv_done, pair(2 * KEYB, KEYB * (h - 1)))
                load_values(sp, values_d, values, h % 2, pair.number(2, h), values_landed)

            def load_m_rows(pair, h):
                wait(sp, m_ready, pair(2, h + 1))
                for i in range(3):
                    row = q_exp[ROWS + i:ROWS + i + 1, h % 2, :].rearrange("a (c q s) -> a q c s", q=4, s=32)
                    for q in range(4):
                        sp.dma_start(row[:, q], m_parts[32 * q:32 * q + KEYB, h % 2, i, :]
                                     ).then_inc(mrow_landed[h % 2], 16)

            def body(pair, attention, experts, tail):
                if experts:
                    wait(sp, S["b2_ps"], pair(1, -1))
                    for h in range(2):
                        sp.dma_start(x_in[64 * h:64 * h + 64], x_pairs[pair.number(1, -1), h]
                                     ).then_inc(S["xin_landed"], 16)
                last = isinstance(pair.p, int) and pair.p == PAIRS - 1
                if attention:
                    if not last:
                        load_for_max(pair, 2)
                    load_for_exp(pair, 1)
                    load_m_rows(pair, 1)
                if tail:
                    wait(sp, S["out_done"], pair(1, -1))
                    for h in range(2):
                        sp.dma_start(out_pairs[pair.number(1, -2), h], out_sb[64 * h:64 * h + 64]
                                     ).then_inc(out_stored, 16)
                if attention:
                    if not last:
                        load_for_max(pair, 3)
                        load_for_exp(pair, 2)
                        load_m_rows(pair, 2)

            start = Pair(sp, 0)
            load_for_exp(start, 0)
            load_for_max(start, 1)
            load_m_rows(start, 0)
            over_pairs(sp, body)
            sp.wait_ge(out_stored, 32 * PAIRS)

        @block.tensor
        def _(pe):
            def max_block(pair, s):
                head, par = s // HSTEPS, s // HSTEPS % 2
                c, j = s % HSTEPS // QC, s % QC
                if s % HSTEPS == 0:
                    wait(pe, max_landed[par], pair(STACK_SEM, STACK_SEM * (head // 2 + 1)))
                wait(pe, max_done, pair(STEPS, s - (3 if beside_nothing(pair) else 1)))
                nc.tensor.matmul(max_bank(pair, s)[:], q_max[0:ROWS, par, P * c:P * c + P],
                                 k_max[0:ROWS, par, 512 * j:512 * j + 512], start=True,
                                 stop=True).then_inc(max_ps, 1)

            def score_block(pair, s):
                par, t, j = s // HSTEPS, s % HSTEPS // QC, s % QC
                if s % HSTEPS == 0:
                    wait(pe, exp_landed[par], pair(STACK_SEM, STACK_SEM))
                    wait(pe, mrow_landed[par], pair(MROW_SEM, MROW_SEM))
                banks = score_banks(pair)
                wait(pe, probs_done, pair(STEPS, s - len(banks) + 1))
                nc.tensor.matmul(banks[s % len(banks)][:], k_exp[0:ROWS + 3, par, P * t:P * t + P],
                                 q_exp[0:ROWS + 3, par, 512 * j:512 * j + 512], start=True,
                                 stop=True).then_inc(score_ps, 1)

            def value_products(pair, k):
                par, t = k // KEYB % 2, k % KEYB
                if t == 0:
                    wait(pe, values_landed[par], pair(16, 16))
                    wait(pe, o_done, pair(2, k // KEYB))
                wait(pe, probs_done, pair(STEPS, QC * k + QC))
                for j in range(QC):
                    last = nc.tensor.matmul(ps_o[VW * j:VW * j + VW, :], values[:, par, t, :],
                                            probs[:, k % 2, j, :], start=(t == 0), stop=(t == KEYB - 1),
                                            tile_position=(0, VW * j))
                last.then_inc(pv_done, 1)

            def product(ps, wh, wl, ah, al, start, stop):
                nc.tensor.matmul(ps, wh, ah, start=start, stop=False)
                nc.tensor.matmul(ps, wl, ah, start=False, stop=False)
                return nc.tensor.matmul(ps, wh, al, start=False, stop=stop)

            def tile_products(f, t, back):
                def at(each, more):
                    return f(each, more - back * each)

                n, kind = (t - FIRST) // PER_TILE, (t - FIRST) % PER_TILE
                if 0 <= n < FT and kind == 1:
                    e, c = n // HC, P * (n % HC)
                    if n == 0:
                        wait(pe, S["h_moved"], at(1, 1))
                        wait(pe, S["l_moved"], at(1, 1))
                        if isinstance(f.p, int) and f.p == 1:
                            wait(pe, w_done, 3 * EXPERTS)
                    second = alone(f, back, n - 1)
                    wait(pe, S["gate_done"], at(FT, n - second))
                    product(gate_bank(f, back, n)[:], w_h[1][:, e, c:c + P], w_l[1][:, e, c:c + P], xt_h[:], xt_l[:],
                            True, True).then_inc(S["gate_ps"], 1)
                if 0 <= n < FT and kind == 3:
                    e, c = n // HC, P * (n % HC)
                    reader = {3: ("out_done", at(1, 0)), 4: ("y_init", at(1, 1))}
                    reader.update({HC * i + 2: ("bcast_done", at(EXPERTS, i + 1)) for i in range(EXPERTS)})
                    if alone(f, back, n):
                        reader = {}
                    else:
                        reader.update({(STEPS + step - FIRST) // PER_TILE: user for step, user in (
                            (5, ("att_done", at(2, 3))), (9, ("att_done", at(2, 4))), (21, ("xtl_done", at(1, 2))),
                            (25, ("lsum_done", at(1, 2))), (37, ("comb_t_done", at(1, 2))))})
                    if n in reader:
                        wait(pe, S[reader[n][0]], reader[n][1])
                    wait(pe, S["hid_done"], at(FT, n - alone(f, back, n - 1)))
                    product(up_bank(f, back, n)[:], w_h[0][:, e, c:c + P], w_l[0][:, e, c:c + P], xt_h[:], xt_l[:],
                            True, True).then_inc(S["up_ps"], 1)
                m = down_tile(f, t, back)
                if m is not None:
                    e, c = m // HC, m % HC
                    if c == 0:
                        by_vector = alone(f, back, m) if e else alone(f, back + 1, FT)
                        second = alone(f, back, m - HC) if e else alone(f, back + 1, FT - HC)
                        wait(pe, S["y_scaled_done" if by_vector else "y_copied"], at(EXPERTS, e - second))
                    wait(pe, S["lo_done"], at(FT, m + 1))
                    product(y_bank(f, back, e)[:], w_h[2][:, e, P * c:P * c + P], w_l[2][:, e, P * c:P * c + P],
                            hid_h[:, m % 2, :], hid_l[:, m % 2, :], c == 0, c == HC - 1).then_inc(S["y_ps"], 1)

            def other_products(f, t, back):
                def at(each, more):
                    return f(each, more - back * each)

                ps = other_bank(f)

                def bank_is_free():
                    if ps is ps_u:
                        wait(pe, S["hid_done"], at(FT, (t - FIRST) // PER_TILE))
                    elif t % STEPS in other_readers[f.p]:
                        name, count = other_readers[f.p][t % STEPS]
                        wait(pe, S[name], count)
                    else:
                        wait(pe, probs_done, STEPS * PAIRS)

                if t in (5, 9):
                    half = (t - 5) // 4
                    bank_is_free()
                    wait(pe, o_done, at(2, 2))
                    if half:
                        wait(pe, S["att_done"], at(2, 1))
                    turned = o_sb[:].rearrange("p h (q a) -> p a h q", a=8)
                    for a in range(4):
                        last = nc.tensor.transpose(ps[:, P * a:P * a + P], turned[:, 4 * half + a], ident[:])
                    last.then_inc(S["o_turned"], 1)
                if t == 21:
                    bank_is_free()
                    wait(pe, S["xhat_done"], at(4, 4))
                    for c in range(4):
                        last = nc.tensor.transpose(ps[:, P * c:P * c + P], x_hat[:, c, :], ident[:])
                    last.then_inc(S["xt_ps"], 1)
                if t == 25:
                    bank_is_free()
                    wait(pe, S["xth_done"], at(1, 1))
                    wait(pe, S["xtl_done"], at(1, 1))
                    for c in range(4):
                        for i, a in enumerate((next_h, next_l)):
                            last = nc.tensor.matmul(ps[:, 2 * EXPERTS * c:2 * EXPERTS * (c + 1)],
                                                    a[:, P * c:P * c + P], wg_hl[:].rearrange("p w e -> p (w e)"),
                                                    start=(i == 0), stop=(i == 1))
                    last.then_inc(S["logit_ps"], 1)
                if t == 37:
                    bank_is_free()
                    wait(pe, S["comb_done"], at(1, 1))
                    for c in range(4):
                        last = nc.tensor.transpose(ps[0:EXPERTS, P * c:P * c + P], comb[:, c, :], ident[:])
                    last.then_inc(S["comb_ps"], 1)
                e = (t - FIRST - 9) // 16
                if 0 <= e < EXPERTS and (t - FIRST) % 16 == 9:
                    bank_is_free()
                    wait(pe, S["comb3_done"], at(2, 2))
                    nc.tensor.matmul(ps[:], sel[:, e, :], comb3[:], start=True, stop=True
                                     ).then_inc(S["bcast_ps"], 1)
                if t == FIRST + 17:
                    bank_is_free()
                    nc.tensor.matmul(ps[:], b2_sb[:], comb_t, start=True, stop=True).then_inc(S["b2_ps"], 1)
                if t == FIRST + 13 + STEPS:
                    bank_is_free()
                    wait(pe, S["y_done"], at(EXPERTS, EXPERTS))
                    for c in range(4):
                        last = nc.tensor.transpose(ps[:, P * c:P * c + P], y_sum[:, P * c:P * c + P], ident[:])
                    last.then_inc(S["final_ps"], 1)

            def body(pair, attention, experts, tail):
                if isinstance(pair.p, int) and pair.p == PAIRS:
                    wait(pe, max_done, STEPS * PAIRS)
                for s in range(STEPS):
                    if attention:
                        score_block(pair, s)
                        if has_max(pair, s):
                            max_block(pair, s + AHEAD)
                    late = s - 1 if beside_nothing(pair) else s
                    if late % QC == 0 and (late > 0 and attention or late == 0 and experts):
                        value_products(pair, late // QC - 1)
                    for step in (tile_products, other_products):
                        if tail:
                            step(pair, s + STEPS, 2)
                        if experts:
                            step(pair, s, 1)

            for s in range(EARLY, AHEAD):
                max_block(Pair(pe, 0), s)
            over_pairs(pe, body)

        @block.scalar
        def _(act):
            def exponentials(pair, s):
                k, j = s // QC, s % QC
                wait(act, score_ps, pair(STEPS, s + 1))
                if j == 0:
                    wait(act, pv_done, pair(2 * KEYB, k - 1))
                banks = score_banks(pair)
                nc.scalar.activation(probs[:, k % 2, j, :], banks[s % len(banks)][:], ACT.Exp).then_inc(probs_done, 1)

            def copy_sums(pair, h):
                wait(act, pv_done, pair(2 * KEYB, KEYB * (h + 1)))
                wait(act, S["o_turned"], pair(2, 0 if h == 0 else -2))
                nc.scalar.activation(o_sb[:, h % 2, :], ps_o[:], ACT.Copy).then_inc(o_done, 1)

            def before_exponential(f, t, back):
                def at(each, more):
                    return f(each, more - back * each)

                if t == 22:
                    wait(act, S["xt_ps"], at(1, 1))
                    wait(act, S["h_moved"], at(1, 0))
                    nc.scalar.activation(next_h[:], other_bank(f)[:], ACT.Copy).then_inc(S["xth_done"], 1)
                n, kind = (t - FIRST) // PER_TILE, (t - FIRST) % PER_TILE
                if 0 <= n < FT and kind == 2:
                    wait(act, S["gate_ps"], at(FT, n + 1))
                    wait(act, S["lo_done"], at(FT, n - 3))
                    nc.scalar.activation(hid[:, n % 4, :], gate_bank(f, back, n)[:], ACT.Tanh, bias=b1h_c[:, n:n + 1],
                                         scale=0.5)
                e = (t - FIRST - 10) // 16
                if 0 <= e < EXPERTS and (t - FIRST) % 16 == 10:
                    wait(act, S["bcast_ps"], at(EXPERTS, e + 1))
                    wait(act, S["y_scaled_done"], at(EXPERTS, e - 1))
                    nc.scalar.activation(comb_b[:, e % 2, :], other_bank(f)[:], ACT.Copy, scale=0.5
                                         ).then_inc(S["bcast_done"], 1)
                if t == FIRST:
                    wait(act, S["up_ps"], at(FT, 0))
                    wait(act, S["xtl_done"], at(1, 1))
                    nc.scalar.activation(xt_l[:], next_l[:], ACT.Copy).then_inc(S["l_moved"], 1)
                if t == FIRST + 18:
                    wait(act, S["b2_ps"], at(1, 1))
                    act.wait_ge(w_done, 3 * EXPERTS)
                    nc.scalar.activation(y_sum, other_bank(f)[:], ACT.Copy).then_inc(S["y_init"], 1)

            def after_exponential(f, t, back):
                def at(each, more):
                    return f(each, more - back * each)

                n, kind = (t - FIRST) // PER_TILE, (t - FIRST) % PER_TILE
                if 0 <= n < FT and kind == 3:
                    wait(act, S["silu_done"], at(FT, n - 1))
                    nc.scalar.activation(gate[:, n % 2, :], gate_bank(f, back, n)[:], ACT.Identity, bias=b1_c[:, n:n + 1]
                                         ).then_inc(S["gate_done"], 1)
                n -= 1
                by_scalar = not alone(f, back, n + 1) and kind == 1 or scalar_splits(f, back, n) and kind == 3
                if 0 <= n < FT and by_scalar:
                    wait(act, S["hid_done"], at(FT, n + 1))
                    wait(act, S["y_ps"], at(FT, n - 1))
                    nc.scalar.activation(hid_h[:, n % 2, :], hid[:, n % 4, :], ACT.Copy).then_inc(S["hi_done"], 1)
                e = expert_summed(f, t, back)
                if e is not None and not alone(f, back, HC * (e + 1)):
                    wait(act, S["y_ps"], at(FT, HC * (e + 1)))
                    wait(act, S["y_done"], at(EXPERTS, e))
                    nc.scalar.activation(y_scaled, ps_y[:], ACT.Copy).then_inc(S["y_copied"], 1)
                if t == 31:
                    wait(act, S["gap_done"], at(1, 1))
                    nc.scalar.activation(gap_exp[:], gap[:], ACT.Exp).then_inc(S["gexp_done"], 1)
                if t == 100:
                    wait(act, S["xres_done"], at(1, 1))
                    wait(act, out_stored, at(32, 0))
                    nc.scalar.activation(out_sb[:], x_res[:], ACT.Copy).then_inc(S["base_done"], 1)

            def body(pair, attention, experts, tail):
                for s in range(STEPS):
                    if experts:
                        before_exponential(pair, s, 1)
                    if tail:
                        before_exponential(pair, s + STEPS, 2)
                    if attention:
                        exponentials(pair, s)
                    if tail:
                        after_exponential(pair, s + STEPS, 2)
                    if experts:
                        after_exponential(pair, s, 1)
                    if s == 0 and experts:
                        copy_sums(pair, -1)
                    if s == HSTEPS + beside_nothing(pair) and attention:
                        copy_sums(pair, 0)

            over_pairs(act, body)

        @block.vector
        def _(dve):
            def max_step(pair, s):
                head, c, j = s // HSTEPS, s % HSTEPS // QC, s % QC
                par = head % 2
                wait(dve, max_ps, pair(STEPS, s + 1))
                if s % HSTEPS == 0:
                    wait(dve, fold_done, pair(2, head - 1))
                nc.vector.tensor_reduce(blockmax[:, par, c, j:j + 1], max_bank(pair, s)[:], AX.X,
                                        ALU.max).then_inc(max_done, 1)

            def row_maxima(pair, head, step):
                par = head % 2
                if step == 0:
                    wait(dve, max_done, pair(STEPS, HSTEPS * (head + 1)))
                    wait(dve, fold_t, pair(2, head))
                    nc.vector.tensor_reduce(rowmax[:, 0:KEYB], blockmax[:, par], AX.X, ALU.max).then_inc(fold_done, 1)
                if step == 1:
                    wait(dve, fold_done, pair(2, head + 1))
                    wait(dve, neg_done, pair(2, head))
                    nc.vector.transpose(rowmax_t[:], rowmax[:]).then_inc(fold_t, 1)
                if step == 2:
                    wait(dve, fold_t, pair(2, head + 1))
                    wait(dve, negr_done, pair(2, head))
                    nc.vector.tensor_scalar(negmax[:], rowmax_t[:], -1.0, None, ALU.mult).then_inc(neg_done, 1)
                if step == 3:
                    wait(dve, neg_done, pair(2, head + 1))
                    wait(dve, mrow_landed[par], pair(MROW_SEM, MROW_SEM * (head // 2)))
                    nc.vector.tensor_copy(m_parts[:, par, 0, :], negmax[:]).then_inc(m1_done, 1)
                if step == 4:
                    wait(dve, m1_done, pair(2, head + 1))
                    wait(dve, m_ready, pair(2, head))
                    nc.vector.tensor_tensor(negmax_r[:], negmax[:], m_parts[:, par, 0, :],
                                            ALU.subtract).then_inc(negr_done, 1)
                if step == 5:
                    wait(dve, negr_done, pair(2, head + 1))
                    nc.vector.tensor_copy(m_parts[:, par, 1, :], negmax_r[:]).then_inc(m2_done, 1)
                if step == 6:
                    wait(dve, m2_done, pair(2, head + 1))
                    nc.vector.tensor_tensor(m_parts[:, par, 2, :], negmax_r[:], m_parts[:, par, 1, :],
                                            ALU.subtract).then_inc(m_ready, 1)

            def per_tile(v):
                return v[:].unsqueeze(2).to_broadcast([P, 4, EXPERTS])

            def expert_steps(f, t, back):
                def at(each, more):
                    return f(each, more - back * each)

                def after(name, each=1, more=1):
                    wait(dve, S[name], at(each, more))

                vec = nc.vector
                tt, ts = nc.vector.tensor_tensor, nc.vector.tensor_scalar
                if t in (13, 14):
                    after("xres_done")
                    for c in (0, 1) if t == 13 else (2, 3):
                        vec.bn_stats(stats[:, c, :], x_res[:, c, :]).then_inc(S["st_done"], 1)
                if t == 15:
                    for c in range(4):
                        last = vec.bn_aggr(mv[:, c, :], stats[:, c, :])
                    last.then_inc(S["mv_done"], 1)
                if t == 16:
                    after("mv_done")
                    ts(ve[:], mv[:, :, 1], EPS, None, ALU.add).then_inc(S["ve_done"], 1)
                if t in (18, 19):
                    after("rs_done")
                    for c in (0, 1) if t == 18 else (2, 3):
                        ts(x_hat[:, c, :], x_res[:, c, :], mv[:, c, 0:1], rstd[:, c:c + 1],
                           ALU.subtract, ALU.mult).then_inc(S["xhat_done"], 1)
                if t == 22:
                    after("xth_done")
                    after("l_moved", 1, 0)
                    tt(next_l[:], other_bank(f)[:], next_h[:].bitcast(F32), ALU.subtract).then_inc(S["xtl_done"], 1)
                if t == 26:
                    after("lsum_done")
                    tt(logits[:], logits[:], bg_b[:].unsqueeze(1).to_broadcast([P, 4, EXPERTS]),
                       ALU.add).then_inc(S["logit_done"], 1)
                if t == 27:
                    after("top1_done")
                    tt(hit1[:], logits[:], per_tile(top1), ALU.is_equal).then_inc(S["hit1_done"], 1)
                if t == 28:
                    after("pick1_done")
                    vec.tensor_reduce(rank1[:], sel1[:], AX.X, ALU.max).then_inc(S["rank1_done"], 1)
                if t == 29:
                    after("sel1_done")
                    vec.scalar_tensor_tensor(out=rest[:], in0=hit1[:], scalar=-3.0e38, in1=logits[:],
                                             op0=ALU.mult, op1=ALU.add).then_inc(S["rest_done"], 1)
                if t == 30:
                    after("top2_done")
                    tt(gap[:], top2[:], top1[:], ALU.subtract).then_inc(S["gap_done"], 1)
                    tt(hit2[:], rest[:], per_tile(top2), ALU.is_equal).then_inc(S["hit2_done"], 1)
                if t == 31:
                    after("pick2_done")
                    vec.tensor_reduce(rank2[:], sel2[:], AX.X, ALU.max).then_inc(S["rank2_done"], 1)
                if t == 33:
                    after("gsum_done")
                    vec.reciprocal(gate1[:], gate_sum[:]).then_inc(S["gate1_done"], 1)
                if t == 34:
                    after("gate2_done")
                    after("sel2_done")
                    tt(sel2[:], hit2[:], per_tile(gate2), ALU.mult).then_inc(S["mix2_done"], 1)
                if t == 42:
                    after("comb_t_done")
                    after("bcast_ps", EXPERTS, 0)
                    vec.tensor_copy(comb3[0:EXPERTS, :], comb_t).then_inc(S["comb1_done"], 1)
                if t == 44:
                    after("comb_r_done")
                    vec.tensor_copy(comb_m[:], comb_r[:]).then_inc(S["comb2_done"], 1)
                if t == 45:
                    after("comb2_done")
                    vec.tensor_copy(comb3[32:32 + EXPERTS, :], comb_m[:]).then_inc(S["comb3_done"], 1)
                if t == 46:
                    tt(comb3[64:64 + EXPERTS, :], comb_r[:], comb_m[:], ALU.subtract).then_inc(S["comb3_done"], 1)


            def before_max(f, t, back):
                def at(each, more):
                    return f(each, more - back * each)

                def after(name, each=1, more=1):
                    wait(dve, S[name], at(each, more))

                vec = nc.vector
                tt, ts = nc.vector.tensor_tensor, nc.vector.tensor_scalar
                if t == FIRST:
                    after("up_ps", FT, 0)
                    after("xth_done")
                    vec.tensor_copy(xt_h[:], next_h[:]).then_inc(S["h_moved"], 1)
                n, kind = (t - FIRST) // PER_TILE - 1, (t - FIRST) % PER_TILE
                if 0 <= n < FT and kind == 0:
                    after("gate_done", FT, n + 1)
                    vec.scalar_tensor_tensor(out=hid[:, n % 4, :], in0=hid[:, n % 4, :], scalar=1.0,
                                             in1=gate[:, n % 2, :], op0=ALU.add, op1=ALU.mult
                                             ).then_inc(S["silu_done"], 1)
                    after("up_ps", FT, n + 1)
                    after("silu_done", FT, n + 1)
                    vec.scalar_tensor_tensor(out=hid[:, n % 4, :], in0=up_bank(f, back, n)[:], scalar=b0_c[:, n:n + 1],
                                             in1=hid[:, n % 4, :], op0=ALU.add, op1=ALU.mult
                                             ).then_inc(S["hid_done"], 1)
                if 0 <= n < FT and kind == 0 and alone(f, back, n + 1) and not scalar_splits(f, back, n):
                    after("hid_done", FT, n + 1)
                    after("y_ps", FT, n - 1)
                    vec.tensor_copy(hid_h[:, n % 2, :], hid[:, n % 4, :]).then_inc(S["hi_done"], 1)
                if t in (6, 10):
                    half = (t - 6) // 4
                    after("o_turned", 2, half + 1)
                    sums = other_bank(f)[:].rearrange("p (a c j) -> p a c j", a=4, j=VW)
                    vec.reciprocal(inv_den[:, 4 * half:4 * half + 4, :], sums[:, :, :, DK]).then_inc(S["den_done"], 1)
                    after("den_done", 2, half + 1)
                    dst = x_hat[:].rearrange("p c (a j) -> p a c j", j=DK)
                    inv = inv_den[:, 4 * half:4 * half + 4, :].unsqueeze(3).to_broadcast([P, 4, 4, DK])
                    tt(dst[:, 4 * half:4 * half + 4], sums[:, :, :, 0:DK], inv, ALU.mult).then_inc(S["att_done"], 1)
                e = expert_summed(f, t, back)
                if e is not None and alone(f, back, HC * (e + 1)):
                    after("y_ps", FT, HC * (e + 1))
                    after("bcast_done", EXPERTS, e + 1)
                    after("y_done", EXPERTS, e)
                    tt(y_scaled, y_bank(f, back, e)[:], comb_b[:, e % 2, :], ALU.mult).then_inc(S["y_scaled_done"], 1)
                if t == 26:
                    after("logit_ps")
                    vec.tensor_reduce(logits[:], other_bank(f)[:, 0:8 * EXPERTS].rearrange("p (c w e) -> p c e w", c=4, w=2),
                                      AX.X, ALU.add).then_inc(S["lsum_done"], 1)
                if t == 27:
                    after("logit_done")
                    vec.tensor_reduce(top1[:], logits[:], AX.X, ALU.max).then_inc(S["top1_done"], 1)
                if t == 28:
                    after("hit1_done")
                    tt(sel1[:], hit1[:], rank[:], ALU.mult).then_inc(S["pick1_done"], 1)
                if t == 29:
                    after("rank1_done")
                    tt(hit1[:], sel1[:], per_tile(rank1), ALU.is_equal).then_inc(S["sel1_done"], 1)
                if t == 30:
                    after("rest_done")
                    vec.tensor_reduce(top2[:], rest[:], AX.X, ALU.max).then_inc(S["top2_done"], 1)
                if t == 31:
                    after("hit2_done")
                    tt(sel2[:], hit2[:], rank[:], ALU.mult).then_inc(S["pick2_done"], 1)
                if t == 32:
                    after("rank2_done")
                    tt(hit2[:], sel2[:], per_tile(rank2), ALU.is_equal).then_inc(S["sel2_done"], 1)
                if t == 33:
                    after("gexp_done")
                    ts(gate_sum[:], gap_exp[:], 1.0, None, ALU.add).then_inc(S["gsum_done"], 1)
                if t == 34:
                    after("gate1_done")
                    tt(gate2[:], gate1[:], gap_exp[:], ALU.mult).then_inc(S["gate2_done"], 1)
                    tt(sel1[:], hit1[:], per_tile(gate1), ALU.mult).then_inc(S["mix1_done"], 1)
                if t == 35:
                    after("mix1_done")
                    after("mix2_done")
                    tt(comb[:], sel1[:], sel2[:], ALU.add).then_inc(S["comb_done"], 1)
                if t == 38:
                    after("comb_ps")
                    vec.tensor_copy(comb_t, other_bank(f)[0:EXPERTS, :]).then_inc(S["comb_t_done"], 1)
                if t == FIRST + 14 + STEPS:
                    after("final_ps")
                    after("base_done")
                    tt(out_sb[:], other_bank(f)[:].rearrange("p (c d) -> p c d", c=4), out_sb[:],
                       ALU.add).then_inc(S["out_done"], 1)

            def fold(pair, s, steps):
                for step in steps:
                    last = s + AHEAD - (step + 1) // 2
                    if last > 0 and last % HSTEPS == HSTEPS - 1 and has_max(pair, last - AHEAD):
                        row_maxima(pair, last // HSTEPS, step)

            def body(pair, attention, experts, tail):
                for s in range(STEPS):
                    if experts:
                        before_max(pair, s, 1)
                    if tail:
                        before_max(pair, s + STEPS, 2)
                    if experts and s == 15:
                        wait(dve, S["st_done"], pair(4, 0))
                    if attention:
                        fold(pair, s, (1, 3, 5))
                        if has_max(pair, s):
                            max_step(pair, s + AHEAD)
                        fold(pair, s, (0, 2, 4, 6))
                    if tail:
                        expert_steps(pair, s + STEPS, 2)
                    if experts:
                        expert_steps(pair, s, 1)

            nc.vector.memset(rowmax[:, KEYB:], 0.0).then_inc(zero_done, 1)
            dve.wait_ge(zero_done, 1)
            start = Pair(dve, 0)
            for s in range(EARLY - AHEAD, 0):
                fold(start, s, (1, 3, 5))
                max_step(start, s + AHEAD)
                fold(start, s, (0, 2, 4, 6))
            over_pairs(dve, body)

        @block.gpsimd
        def _(pool):
            def expert_steps(f, t, back):
                def at(each, more):
                    return f(each, more - back * each)

                if t == 11:
                    wait(pool, S["att_done"], at(2, 2))
                    wait(pool, S["base_done"], at(1, 0))
                    wait(pool, S["xin_landed"], at(32, 32))
                    nc.gpsimd.tensor_tensor(x_res[:], x_hat[:], x_in[:], ALU.add).then_inc(S["xres_done"], 1)
                if t == 16:
                    wait(pool, S["ve_done"], at(1, 1))
                    nc.gpsimd.tensor_tensor(rstd[:], ve[:], exponent[:, 0:4], ALU.pow).then_inc(S["rs_done"], 1)
                if t == 42:
                    wait(pool, S["comb1_done"], at(1, 1))
                    nc.gpsimd.tensor_tensor(comb_r[:], comb_t, comb3[0:EXPERTS, :], ALU.subtract
                                            ).then_inc(S["comb_r_done"], 1)
                n = (t - FIRST) // PER_TILE - 1
                if 0 <= n < FT and (t - FIRST) % PER_TILE == 1:
                    wait(pool, S["hi_done"], at(FT, n + 1))
                    nc.gpsimd.tensor_tensor(hid_l[:, n % 2, :], hid[:, n % 4, :], hid_h[:, n % 2, :].bitcast(F32),
                                            ALU.subtract).then_inc(S["lo_done"], 1)
                e = expert_summed(f, t, back)
                if e is not None:
                    if not alone(f, back, HC * (e + 1)):
                        wait(pool, S["y_copied"], at(EXPERTS, e + 1))
                        wait(pool, S["bcast_done"], at(EXPERTS, e + 1))
                        nc.gpsimd.tensor_tensor(y_scaled, y_scaled, comb_b[:, e % 2, :], ALU.mult
                                                ).then_inc(S["y_scaled_done"], 1)
                    wait(pool, S["y_scaled_done"], at(EXPERTS, e + 1))
                    wait(pool, S["y_done"], at(EXPERTS, e))
                    if e == 0:
                        wait(pool, S["y_init"], at(1, 1))
                    nc.gpsimd.tensor_tensor(y_sum, y_sum, y_scaled, ALU.add).then_inc(S["y_done"], 1)

            def body(pair, attention, experts, tail):
                for s in range(STEPS):
                    if experts:
                        expert_steps(pair, s, 1)
                    if tail:
                        expert_steps(pair, s + STEPS, 2)

            def load(i):
                w, e = i // EXPERTS, i % EXPERTS
                if i >= 2:
                    pool.wait_ge(w_done, i - 1)
                src = (W0[e], W1[e], W2[e].rearrange("(c p) d -> p c d", p=P))[w]
                dst = w_raw[:, i % 2, :]
                if w == 2:
                    dst = dst.rearrange("p (c d) -> p c d", c=HC)
                pool.dma_start(dst, src).then_inc(w_landed[i % 2], 16)

            load(0)
            for i in range(3 * EXPERTS):
                if i + 1 < 3 * EXPERTS:
                    load(i + 1)
                w, e = i // EXPERTS, i % EXPERTS
                pool.wait_ge(w_landed[i % 2], 16 * (i // 2 + 1))
                nc.gpsimd.tensor_scalar(w_h[w][:, e, :], w_raw[:, i % 2, :], 1.0, 0.0, ALU.mult,
                                        ALU.add).then_inc(wh_done, 1)
                pool.wait_ge(wh_done, i + 1)
                nc.gpsimd.tensor_tensor(w_l[w][:, e, :], w_raw[:, i % 2, :], w_h[w][:, e, :].bitcast(F32),
                                        ALU.subtract).then_inc(w_done, 1)
            over_pairs(pool, body)


def block_kernel(nc, x, Wq, bq, Wk, bk, Wv, bv, gamma, beta, Wg, bg, W0, b0, W1, b1, W2, b2, out):
    parts_d = nc.dram_tensor("parts_scratch", [2, NHEADS, 3, DK, SEQ], BF16).ap()
    values_d = nc.dram_tensor("values_scratch", [BATCH, HEADS, P, KEYB * VW], F32).ap()
    with ExitStack() as ctx:
        def sb(name, shape, dt=F32):
            return ctx.enter_context(nc.sbuf_tensor(name, shape, dt))

        keep = (sb("ident", [P, P]), sb("rank", [P, 4, EXPERTS]), sb("bg_b", [P, EXPERTS]),
                sb("wg_hl", [P, 2, EXPERTS], F32R),
                sb("b0_c", [P, FT]), sb("b1_c", [P, FT]), sb("b1h_c", [P, FT]),
                sb("b2_sb", [EXPERTS, D]), sb("sel", [96, EXPERTS, P], BF16), sb("comb3", [96, 512], BF16),
                sb("exponent", [P, 4]))
        stacks = (sb("q_max", [P, 2, SEQ], BF16), sb("k_max", [P, 2, SEQ], BF16),
                  sb("q_exp", [P, 2, SEQ], BF16), sb("k_exp", [P, 2, SEQ], BF16),
                  sb("values", [P, 2, KEYB, VW]), sb("blockmax", [P, 2, KEYB, QC]),
                  ctx.enter_context(nc.semaphore("max_ps")), ctx.enter_context(nc.semaphore("max_done")),
                  *[[ctx.enter_context(nc.semaphore(f"{name}_landed{i}")) for i in range(2)]
                    for name in ("max", "exp", "values")])
        setup_stage(nc, (x, Wq, bq, Wk, bk, Wv, bv, gamma, beta, Wg, bg, b0, b1, b2), (parts_d, values_d), keep,
                    stacks)
        main_stage(nc, x, (W0, W1, W2), out, (parts_d, values_d), keep, stacks)


_INS = ["L0_attn_x", "L0_attn_Wq", "L0_attn_bq", "L0_attn_Wk", "L0_attn_bk", "L0_attn_Wv", "L0_attn_bv",
        "L0_attn_gamma", "L0_attn_beta", "L0_ffn_Wg", "L0_ffn_bg", "L0_ffn_W0", "L0_ffn_b0", "L0_ffn_W1",
        "L0_ffn_b1", "L0_ffn_W2", "L0_ffn_b2"]


def kernel(**inputs):
    import numpy as _np
    import concourse.bacc as _bacc
    from concourse import mybir as _mybir
    from concourse.bass_utils import run_bass_kernel_spmd as _run

    nc = _bacc.Bacc("TRN2", target_bir_lowering=False, num_devices=1)
    arrays, args = {}, []
    for name in _INS:
        a = _np.ascontiguousarray(inputs[name])
        arrays[f"in_{name}_dram"] = a
        args.append(nc.dram_tensor(f"in_{name}_dram", a.shape, _mybir.dt.from_np(a.dtype), kind="ExternalInput").ap())
    out = nc.dram_tensor("out_dram", (BATCH, SEQ, D), F32, kind="ExternalOutput").ap()
    block_kernel(nc, *args, out)
    r = _run(nc, [arrays], core_ids=[0])
    return r.results[0]["out_dram"]
```
